# Optimizing a Trainium2 kernel written in Bass

```python
import numpy as np
import jax
import jax.numpy as jnp

def _softmax(x, axis=-1):
    return jax.nn.softmax(x, axis=axis)

def _gelu(x):
    return jax.nn.gelu(x, approximate=True)

def _silu(x):
    return jax.nn.silu(x)

def _sigmoid(x):
    return jax.nn.sigmoid(x)

def _layernorm(x, axis=-1, eps=1e-05):
    m = jnp.mean(x, axis=axis, keepdims=True)
    v = jnp.var(x, axis=axis, keepdims=True)
    return (x - m) / jnp.sqrt(v + eps)

def _scatter_add(tgt, idx, src, axis=0):
    return tgt.at[idx].add(src)

def _segment_sum(src, seg, n):
    return jax.ops.segment_sum(src, seg, n)
kernel_name = 'mk_early_fusion_d1_tok_img768_r4_749f57'

def setup_inputs(seed: int=0):
    np.random.seed(seed)
    _w = jnp.asarray

    def _rec_inputs():
        import jax
        import jax.numpy as jnp
        _rk = jax.random.key(seed)
        x = 7.57192e-06 + 1.00007 * jax.random.normal(jax.random.fold_in(_rk, 1), (64, 3, 224, 224), jnp.float32)
        txt = 1.59752e-10 + 0.999997 * jax.random.normal(jax.random.fold_in(_rk, 2), (64, 32, 192), jnp.float32)
        return (x, txt)
    x, txt = _rec_inputs()

    def _L0_tok_setup():
        import jax, jax.numpy as jnp
        import numpy as np
        IMG, P, C, E = (224, 16, 3, 192)
        OFFSETS = [(0, 4), (4, 0), (0, -4), (-4, 0)]
        NSHIFT = 1 + len(OFFSETS)
        D = P * P * C * NSHIFT
        LN_EPS = 1e-05

        def _shifted(x, dx, dy):
            y = jnp.roll(x, shift=(dx, dy), axis=(2, 3))
            if dx > 0:
                y = y.at[:, :, :dx, :].set(0.0)
            elif dx < 0:
                y = y.at[:, :, dx:, :].set(0.0)
            if dy > 0:
                y = y.at[:, :, :, :dy].set(0.0)
            elif dy < 0:
                y = y.at[:, :, :, dy:].set(0.0)
            return y
        key = jax.random.key(seed)
        k1, k2 = jax.random.split(key)
        x = jax.random.normal(k1, (64, C, IMG, IMG), dtype=jnp.float32)
        proj_w = jax.random.normal(k2, (E, D), dtype=jnp.float32) * 0.02
        proj_b = jnp.zeros((E,), dtype=jnp.float32)
        gamma = jnp.ones((E,), dtype=jnp.float32)
        beta = jnp.zeros((E,), dtype=jnp.float32)
        return {'x': x, 'proj_w': proj_w, 'proj_b': proj_b, 'gamma': gamma, 'beta': beta}
    _L0_tok_all = _L0_tok_setup()
    _L0_tok_in = {k: v for k, v in _L0_tok_all.items() if k in ('proj_w', 'proj_b', 'gamma', 'beta')}
    del _L0_tok_all

    def _L0_attn_setup():
        import jax, jax.numpy as jnp
        import numpy as np
        DIM = 192
        NUM_HEADS = 12
        HEAD_DIM = DIM // NUM_HEADS
        SCALE = HEAD_DIM ** (-0.5)
        B, N = (4, 512)
        key = jax.random.key(seed)
        k1, k2, k3, k4 = jax.random.split(key, 4)
        x = jax.random.normal(k1, (B, N, DIM), dtype=jnp.float32)
        Wq = jax.random.normal(k2, (DIM, DIM), dtype=jnp.float32) * DIM ** (-0.5)
        Wkv = jax.random.normal(k3, (2 * DIM, DIM), dtype=jnp.float32) * DIM ** (-0.5)
        Wproj = jax.random.normal(k4, (DIM, DIM), dtype=jnp.float32) * DIM ** (-0.5)
        return {'x': x, 'Wq': Wq, 'Wkv': Wkv, 'Wproj': Wproj}
    _L0_attn_all = _L0_attn_setup()
    _L0_attn_in = {k: v for k, v in _L0_attn_all.items() if k in ('Wq', 'Wkv', 'Wproj')}
    del _L0_attn_all

    def _L0_ffn_setup():
        import jax, jax.numpy as jnp
        import numpy as np
        B, S, H, D, E = (4, 512, 192, 256, 8)
        TOP_K = 2
        EPS = 1e-08
        LN_EPS = 1e-05

        def _gelu(t):
            return jax.nn.gelu(t, approximate=False)

        def _layer_norm(t, gamma, beta):
            mu = jnp.mean(t, axis=-1, keepdims=True)
            var = jnp.mean(jnp.square(t - mu), axis=-1, keepdims=True)
            return (t - mu) * jax.lax.rsqrt(var + LN_EPS) * gamma + beta
        key = jax.random.key(seed)
        ks = jax.random.split(key, 8)
        x = jax.random.normal(ks[0], (B, S, H), dtype=jnp.float32)
        w1 = jax.random.normal(ks[1], (H, H // 2), dtype=jnp.float32) * 0.02
        b1 = jnp.zeros((H // 2,), dtype=jnp.float32)
        w2 = jax.random.normal(ks[2], (H // 2, E), dtype=jnp.float32) * 0.02
        b2 = jnp.zeros((E,), dtype=jnp.float32)
        a_dn = float(np.sqrt(6.0 / (H + D)))
        a_up = float(np.sqrt(6.0 / (D + H)))
        down_w = jax.random.uniform(ks[3], (E, H, D), dtype=jnp.float32, minval=-a_dn, maxval=a_dn)
        down_b = jnp.zeros((E, D), dtype=jnp.float32)
        up_w = jax.random.uniform(ks[4], (E, D, H), dtype=jnp.float32, minval=-a_up, maxval=a_up)
        gamma = jnp.ones((H,), dtype=jnp.float32)
        beta = jnp.zeros((H,), dtype=jnp.float32)
        return {'x': x, 'w1': w1, 'b1': b1, 'w2': w2, 'b2': b2, 'down_w': down_w, 'down_b': down_b, 'up_w': up_w, 'gamma': gamma, 'beta': beta}
    _L0_ffn_all = _L0_ffn_setup()
    _L0_ffn_in = {k: v for k, v in _L0_ffn_all.items() if k in ('w1', 'b1', 'w2', 'b2', 'down_w', 'down_b', 'up_w', 'gamma', 'beta')}
    del _L0_ffn_all
    return {'x': x, 'txt': txt, 'L0_tok_proj_w': _L0_tok_in['proj_w'], 'L0_tok_proj_b': _L0_tok_in['proj_b'], 'L0_tok_gamma': _L0_tok_in['gamma'], 'L0_tok_beta': _L0_tok_in['beta'], 'L0_attn_Wq': _L0_attn_in['Wq'], 'L0_attn_Wkv': _L0_attn_in['Wkv'], 'L0_attn_Wproj': _L0_attn_in['Wproj'], 'L0_ffn_w1': _L0_ffn_in['w1'], 'L0_ffn_b1': _L0_ffn_in['b1'], 'L0_ffn_w2': _L0_ffn_in['w2'], 'L0_ffn_b2': _L0_ffn_in['b2'], 'L0_ffn_down_w': _L0_ffn_in['down_w'], 'L0_ffn_down_b': _L0_ffn_in['down_b'], 'L0_ffn_up_w': _L0_ffn_in['up_w'], 'L0_ffn_gamma': _L0_ffn_in['gamma'], 'L0_ffn_beta': _L0_ffn_in['beta']}

def reference(x, txt, L0_tok_proj_w, L0_tok_proj_b, L0_tok_gamma, L0_tok_beta, L0_attn_Wq, L0_attn_Wkv, L0_attn_Wproj, L0_ffn_w1, L0_ffn_b1, L0_ffn_w2, L0_ffn_b2, L0_ffn_down_w, L0_ffn_down_b, L0_ffn_up_w, L0_ffn_gamma, L0_ffn_beta):
    import jax
    import jax.numpy as jnp

    def _L0_tok_ref(x, proj_w, proj_b, gamma, beta):
        import jax, jax.numpy as jnp
        import numpy as np
        IMG, P, C, E = (224, 16, 3, 192)
        OFFSETS = [(0, 4), (4, 0), (0, -4), (-4, 0)]
        NSHIFT = 1 + len(OFFSETS)
        D = P * P * C * NSHIFT
        LN_EPS = 1e-05

        def _shifted(x, dx, dy):
            y = jnp.roll(x, shift=(dx, dy), axis=(2, 3))
            if dx > 0:
                y = y.at[:, :, :dx, :].set(0.0)
            elif dx < 0:
                y = y.at[:, :, dx:, :].set(0.0)
            if dy > 0:
                y = y.at[:, :, :, :dy].set(0.0)
            elif dy < 0:
                y = y.at[:, :, :, dy:].set(0.0)
            return y
        B = x.shape[0]
        gh = IMG // P
        stacked = jnp.concatenate([x] + [_shifted(x, dx, dy) for dx, dy in OFFSETS], axis=1)
        patches = stacked.reshape(B, C * NSHIFT, gh, P, gh, P)
        patches = patches.transpose(0, 2, 4, 3, 5, 1)
        patches = patches.reshape(B, gh * gh, D)
        h = jnp.einsum('bnd,ed->bne', patches, proj_w) + proj_b
        mu = jnp.mean(h, axis=-1, keepdims=True)
        var = jnp.var(h, axis=-1, keepdims=True)
        out = (h - mu) * jax.lax.rsqrt(var + LN_EPS) * gamma + beta
        return out

    def _L0_attn_ref(x, Wq, Wkv, Wproj):
        import jax, jax.numpy as jnp
        import numpy as np
        DIM = 192
        NUM_HEADS = 12
        HEAD_DIM = DIM // NUM_HEADS
        SCALE = HEAD_DIM ** (-0.5)
        B, N = (4, 512)
        b, n, c = x.shape
        h, d = (NUM_HEADS, HEAD_DIM)
        q = (x @ Wq.T).reshape(b, n, h, d)
        kv = (x @ Wkv.T).reshape(b, n, h, 2 * d)
        k, v = (kv[..., :d], kv[..., d:])
        attn = jnp.einsum('bnhd,bmhd->bhnm', q, k) * SCALE
        neg_inf = jnp.finfo(attn.dtype).min
        attn = attn.at[..., 1:, 0].set(neg_inf)
        attn = jax.nn.softmax(attn, axis=-1)
        out = jnp.einsum('bhnm,bmhd->bnhd', attn, v).reshape(b, n, c)
        out = out @ Wproj.T
        return out

    def _L0_ffn_ref(x, w1, b1, w2, b2, down_w, down_b, up_w, gamma, beta):
        import jax, jax.numpy as jnp
        import numpy as np
        B, S, H, D, E = (4, 512, 192, 256, 8)
        TOP_K = 2
        EPS = 1e-08
        LN_EPS = 1e-05

        def _gelu(t):
            return jax.nn.gelu(t, approximate=False)

        def _layer_norm(t, gamma, beta):
            mu = jnp.mean(t, axis=-1, keepdims=True)
            var = jnp.mean(jnp.square(t - mu), axis=-1, keepdims=True)
            return (t - mu) * jax.lax.rsqrt(var + LN_EPS) * gamma + beta
        logits = _gelu(x @ w1 + b1) @ w2 + b2
        routing = jax.nn.softmax(logits, axis=-1)
        topv, topi = jax.lax.top_k(routing, TOP_K)
        sparse = jnp.sum(jax.nn.one_hot(topi, E, dtype=routing.dtype) * topv[..., None], axis=-2)
        sparse = sparse / (jnp.sum(sparse, axis=-1, keepdims=True) + EPS)
        z = _gelu(jnp.einsum('bsh,ehd->bsed', x, down_w) + down_b)
        expert_out = jnp.einsum('bsed,edh->bseh', z, up_w)
        moe_out = jnp.einsum('bseh,bse->bsh', expert_out, sparse)
        return _layer_norm(x + moe_out, gamma, beta)
    h = _L0_tok_ref(x, L0_tok_proj_w, L0_tok_proj_b, L0_tok_gamma, L0_tok_beta)
    h = jnp.concatenate([h, txt], axis=1)
    h = h + _L0_attn_ref(_layernorm(h, axis=-1), L0_attn_Wq, L0_attn_Wkv, L0_attn_Wproj)
    h = h + _L0_ffn_ref(_layernorm(h, axis=-1), L0_ffn_w1, L0_ffn_b1, L0_ffn_w2, L0_ffn_b2, L0_ffn_down_w, L0_ffn_down_b, L0_ffn_up_w, L0_ffn_gamma, L0_ffn_beta)
    return h

_drawn_inputs = setup_inputs


def setup_inputs(seed=0):
    import zlib

    import numpy as np

    out = dict(_drawn_inputs(seed))
    spreads = {'L0_tok_proj_b': (0.0, 0.1),
     'L0_tok_gamma': (1.0, 0.2),
     'L0_tok_beta': (0.0, 0.1),
     'L0_ffn_b1': (0.0, 0.1),
     'L0_ffn_b2': (0.0, 0.1),
     'L0_ffn_down_b': (0.0, 0.355),
     'L0_ffn_gamma': (1.0, 0.2),
     'L0_ffn_beta': (0.0, 0.1)}
    factors = {}
    for name, (base, spread) in spreads.items():
        noise = np.random.default_rng([zlib.crc32(name.encode()), seed]).standard_normal(out[name].shape)
        drawn = base * np.exp(spread * noise) if base else spread * noise
        out[name] = jnp.asarray(drawn.astype(out[name].dtype))
    for name, factor in factors.items():
        out[name] = (out[name] * factor).astype(out[name].dtype)
    return out
```

```python
from contextlib import ExitStack

import concourse.bass as bass
from concourse import mybir

ALU = mybir.AluOpType
ACT = mybir.ActivationFunctionType
AX = mybir.AxisListType
F32 = mybir.dt.float32
F32R = mybir.dt.float32r

P = 128
E = 192
EW = 256
HEADS, HD = 12, 16
PAIRS = HEADS // 2
GRID = 14
NP = GRID * GRID
TXT = 32
PT, TT = NP // 2, TXT // 2
TOK = PT + TT
N = 2 * TOK
KC, KH = 6, 6
LN_EPS = 1e-5
GATE_EPS = 1e-8
SCALE = HD ** -0.5
MASKED = -(2.0 ** 100)
EXPERTS, DFF = 8, 256
MT = EXPERTS * DFF // P
W1N = E // 2


def at_least(eng, sem, count):
    if not isinstance(count, int) or count > 0:
        eng.wait_ge(sem, count)


def stage_attention(nc, B, x_k, txt, w_center, w_halo, tok_b, tok_g, tok_beta, wqk, wv, wproj,
                    ident_d, aug_d, h1_d):
    with ExitStack() as ctx:
        def sb(name, shape, dt=F32):
            return ctx.enter_context(nc.sbuf_tensor(name, shape, dt))

        def psum(name, shape):
            return ctx.enter_context(nc.psum_tensor(name, shape, F32))

        def sem(name):
            return ctx.enter_context(nc.semaphore(name))

        ident = sb("ident", [P, P])
        low_half = sb("low_half", [P, 1])
        neg_half = sb("neg_half", [P, 2])
        eps = sb("eps", [P, 2])
        wait_pad = sb("wait_pad", [P, 1])
        w_tok = sb("w_tok", [P, KC + KH, E])
        w_add = sb("w_add", [P, 4, KC, E])
        tokb = sb("tokb", [P, E])
        tokg = sb("tokg", [P, E])
        tokbeta = sb("tokbeta", [P, E])
        wqk_f = sb("wqk_f", [P, 2, 2 * E])
        wv_f = sb("wv_f", [P, 2, E])
        wp_f = sb("wp_f", [P, 2, E])
        wqk_h, wqk_l = sb("wqk_h", [P, 2, 2 * E], F32R), sb("wqk_l", [P, 2, 2 * E], F32R)
        wv_h, wv_l = sb("wv_h", [P, 2, E], F32R), sb("wv_l", [P, 2, E], F32R)
        wp_h, wp_l = sb("wp_h", [P, 2, E], F32R), sb("wp_l", [P, 2, E], F32R)
        key_rows = sb("key_rows", [1, 2, PAIRS, N])
        query_rows = sb("query_rows", [PAIRS, 2, N])

        xk = [sb(f"xk{b}", [P, KC + KH, GRID, GRID]) for b in range(2)]
        h = [sb(f"tok{b}", [TOK, 2, E]) for b in range(2)]
        xn = [sb(f"xn{b}", [TOK, 2, EW]) for b in range(2)]
        v = [sb(f"v{b}", [TOK, 2, HEADS, HD + 1]) for b in range(2)]
        q_aug = [sb(f"q_aug{b}", [P, PAIRS, N], F32R) for b in range(2)]
        k_aug = [[sb(f"k_aug{b}{e}", [P, PAIRS, N], F32R) for e in range(2)] for b in range(2)]
        probs = [sb(f"probs{b}", [TOK, 2, PAIRS, 2, N]) for b in range(2)]
        h_pre = sb("h_pre", [TOK, 2, E])
        h_nrm = sb("h_nrm", [TOK, 2, E])
        h_gam = sb("h_gam", [TOK, 2, E])
        stats = sb("stats", [TOK, 4, 6])
        mv = sb("mv", [TOK, 4, 2])
        var_eps = sb("var_eps", [TOK, 4])
        rstd = sb("rstd", [TOK, 4])
        x_h, x_l = sb("x_h", [P, 2, N], F32R), sb("x_l", [P, 2, N], F32R)
        o_h, o_l = sb("o_h", [P, 2, N], F32R), sb("o_l", [P, 2, N], F32R)
        qk_c = sb("qk_c", [96, 4, 2, N], F32R)
        maxes = sb("maxes", [TOK, 2, 2, PAIRS])
        neg_max = sb("neg_max", [HEADS, N], F32R)
        o_n = sb("o_n", [TOK, 2, EW])
        r_sum = sb("r_sum", [TOK, 2, HEADS, 1])
        h1 = sb("h1", [TOK, 2, E])

        ps_s = psum("ps_s", [P, 4, 512])
        ps_tok = psum("ps_tok", [P, 512])
        ps_t = psum("ps_t", [P, 512])
        ps_a = psum("ps_a", [P, 512])
        ps_b = psum("ps_b", [P, 512])

        names = """w_load const_ready w_split w_sum
            x_shift tok_done tok_biased stats1 rstd1 nrm1 h_ready stats2 rstd2 xn_once xn_ready
            xn_turned xh_ready xl_ready qk_done qh_ready ql_ready qk_low v_done v_ready
            aug_stored max_scores max_read max_turned max_ready exp_scores exp_done
            av_done recip o_once o_ready o_turned oh_ready ol_ready proj_done h1_ready sums chain zeroed
            const_chain ln_chain""".split()
        s = {n: sem(n) for n in names}
        x_in = [sem(f"x_in{b}") for b in range(2)]
        txt_in = [sem(f"txt_in{b}") for b in range(2)]
        q_in = [sem(f"q_in{b}") for b in range(2)]
        max_in = [sem(f"max_in{b}") for b in range(2)]
        h1_out = sem("h1_out")

        X_DMAS, Q_DMAS = 5, 8

        def scores(b):
            return ps_s[0:TOK, 2 * b:2 * b + 2, 0:2 * N].rearrange("p a (e n) -> p a e n", e=2)

        block = ctx.enter_context(nc.Block())

        @block.sync
        def _(sp):
            def w(dst, src):
                sp.dma_start(dst, src).then_inc(s["w_load"], 16)

            w(ident[:, :], ident_d)
            w(w_tok[:, 0:KC, :], w_center[0].rearrange("(t p) e -> p t e", p=P))
            for i in range(4):
                w(w_add[:, i, :, :], w_center[i + 1].rearrange("(t p) e -> p t e", p=P))
            w(w_tok[:, KC:KC + KH, :], w_halo.rearrange("(t p) e -> p t e", p=P))
            w(tokb[:, :], tok_b)
            w(tokg[:, :], tok_g)
            w(tokbeta[:, :], tok_beta)
            for dst, src in ((wqk_f, wqk), (wv_f, wv), (wp_f, wproj)):
                w(dst[:, 0, :], src[0:P, :])
                w(dst[0:64, 1, :], src[P:E, :])
                w(dst[64:P, 1, :], src[P:E, :])

            sp.wait_ge(s["const_ready"], 8)
            for e in range(2):
                for c in range(2):
                    row = 32 + c
                    sp.dma_start(aug_d[0, e, row],
                                 query_rows[:, c, :]).then_inc(s["w_load"], 16)
                    sp.dma_start(aug_d[1, e, row],
                                 query_rows[:, c, :]).then_inc(s["w_load"], 16)

            def load_image(i, j, b):
                at_least(sp, s["tok_done"], i - 1)
                src = x_k[i]
                sp.dma_start(xk[b][:, 0:KC].rearrange("p t a c -> p t (a c)"),
                             src.rearrange("(t p) g -> p t g", p=P)).then_inc(x_in[b], 16)
                rows = src.rearrange("(cc r) g -> cc r g", r=16)
                cut = NP - GRID
                sp.dma_start(xk[b][:, 9, 1:GRID, :], rows[0:32, 12:16, 0:cut]).then_inc(x_in[b], 16)
                sp.dma_start(xk[b][0:64, 10, 1:GRID, :], rows[32:48, 12:16, 0:cut]).then_inc(x_in[b], 16)
                sp.dma_start(xk[b][64:P, 10, 0:GRID - 1, :], rows[0:16, 0:4, GRID:NP]).then_inc(x_in[b], 16)
                sp.dma_start(xk[b][:, 11, 0:GRID - 1, :], rows[16:48, 0:4, GRID:NP]).then_inc(x_in[b], 16)

            def load_text(i, j, b):
                at_least(sp, s["h1_ready"], i - 1)
                sp.dma_start(h[b][PT:TOK, :, :], txt[i].rearrange("(t p) e -> p t e", p=TT)).then_inc(txt_in[b], 16)

            def store_load_qk(i, j, b):
                sp.wait_ge(s["qh_ready"], 2 * i + 2)
                sp.wait_ge(s["ql_ready"], 2 * i + 2)
                for t in range(4):
                    sp.dma_start(aug_d[b, t, 0:32].rearrange("(l d) p n -> (d p) l n", l=2),
                                 qk_c[:, t].bitcast(F32)).then_inc(s["aug_stored"], 16)
                sp.wait_ge(s["aug_stored"], 64 * (i + 1))
                for e in range(2):
                    r = 64 * e
                    sp.dma_start(q_aug[b][r:r + 16].bitcast(F32), aug_d[b, e, 0:16]).then_inc(q_in[b], 16)
                    sp.dma_start(q_aug[b][r + 16:r + 50].bitcast(F32), aug_d[b, e, 0:34]).then_inc(q_in[b], 16)
                    sp.dma_start(k_aug[b][e][r:r + 16].bitcast(F32), aug_d[b, 2 + e, 16:32]).then_inc(q_in[b], 16)
                    sp.dma_start(k_aug[b][e][r + 16:r + 48].bitcast(F32), aug_d[b, 2 + e, 0:32]).then_inc(q_in[b], 16)

            def place_max(i, j, b):
                sp.wait_ge(s["max_ready"], i + 1)
                for e in range(2):
                    sp.dma_start(q_aug[b][64 * e + 49:64 * e + 50].bitcast(F32), neg_max[e * PAIRS:(e + 1) * PAIRS, :].bitcast(F32)
                                 ).then_inc(max_in[b], 16)

            def store_h1(i, j, b):
                sp.wait_ge(s["h1_ready"], i + 1)
                sp.dma_start(h1_d[i], h1[:, :, :]).then_inc(h1_out, 16)

            sp.wait_ge(s["const_ready"], 8)
            for b in range(2):
                for e in range(2):
                    r = 64 * e + 48
                    for c in range(2):
                        sp.dma_start(k_aug[b][e][r + c:r + c + 1].bitcast(F32),
                                     key_rows[:, c]).then_inc(s["w_load"], 16)
            sp.wait_ge(s["zeroed"], 1)
            load_image(0, 0, 0)
            load_text(0, 0, 0)
            load_image(1, 0, 1)
            load_text(1, 0, 1)

            def step(i, j, b, first=False, last=False):
                if not last:
                    load_image(i + 2, j + 1, b)
                store_load_qk(i, j, b)
                if not first:
                    store_h1(i - 1, j, 1 - b)
                    if not (last and b == 1):
                        load_text(i + 1, j + b, 1 - b)
                place_max(i, j, b)

            step(0, 0, 0, first=True)
            step(1, 0, 1)
            with sp.Fori(1, B // 2 - 1) as j:
                step(2 * j, j, 0)
                step(2 * j + 1, j, 1)
            step(B - 2, B // 2 - 1, 0, last=True)
            step(B - 1, B // 2 - 1, 1, last=True)
            store_h1(B - 1, B // 2 - 1, 1)
            sp.wait_ge(h1_out, 16 * B)

        W_TOTAL = (1 + 1 + 4 + 1 + 3 + 9 + 8 + 8) * 16

        @block.gpsimd
        def _(pool):
            nc.gpsimd.memset(query_rows[:, 0, :], MASKED).then_inc(s["const_chain"], 1)
            pool.wait_ge(s["const_chain"], 1)
            nc.gpsimd.memset(query_rows[:, 0, 0:1], 0.0).then_inc(s["const_ready"], 1)
            nc.gpsimd.memset(query_rows[:, 1, :], 0.0).then_inc(s["const_ready"], 1)
            nc.gpsimd.memset(key_rows[:, 0], 0.0).then_inc(s["const_chain"], 1)
            pool.wait_ge(s["const_chain"], 2)
            nc.gpsimd.memset(key_rows[:, 0, :, 0:1], 1.0).then_inc(s["const_ready"], 1)
            nc.gpsimd.memset(key_rows[:, 1], 1.0).then_inc(s["const_ready"], 1)

            def root1(i):
                pool.wait_ge(s["stats1"], i + 1)
                nc.gpsimd.tensor_tensor(var_eps[0:PT, 0:2], mv[0:PT, 0:2, 1], eps[0:PT, 0:2], ALU.add
                                        ).then_inc(s["ln_chain"], 1)
                pool.wait_ge(s["ln_chain"], 3 * i + 1)
                nc.gpsimd.tensor_tensor(rstd[0:PT, 0:2], var_eps[0:PT, 0:2], neg_half[0:PT, :], ALU.pow
                                        ).then_inc(s["rstd1"], 1)

            def affine(i, j, b):
                pool.wait_ge(s["nrm1"], i + 1)
                nc.gpsimd.tensor_tensor(h_gam[0:PT], h_nrm[0:PT],
                                        tokg[0:PT].unsqueeze(1).broadcast_to([PT, 2, E]), ALU.mult
                                        ).then_inc(s["ln_chain"], 1)
                pool.wait_ge(s["ln_chain"], 3 * i + 2)
                at_least(pool, s["h1_ready"], i - 1)
                nc.gpsimd.tensor_tensor(h[b][0:PT], h_gam[0:PT],
                                        tokbeta[0:PT].unsqueeze(1).broadcast_to([PT, 2, E]), ALU.add
                                        ).then_inc(s["h_ready"], 1)

            def root2(i):
                pool.wait_ge(s["stats2"], i + 1)
                nc.gpsimd.tensor_tensor(var_eps[:, 2:4], mv[:, 2:4, 1], eps[0:TOK, 0:2], ALU.add
                                        ).then_inc(s["ln_chain"], 1)
                pool.wait_ge(s["ln_chain"], 3 * i + 3)
                nc.gpsimd.tensor_tensor(rstd[:, 2:4], var_eps[:, 2:4], neg_half[0:TOK, :], ALU.pow
                                        ).then_inc(s["rstd2"], 1)

            def tokens(i, j, b):
                root1(i)
                affine(i, j, b)
                root2(i)

            pool.wait_ge(s["zeroed"], 1)
            tokens(0, 0, 0)
            tokens(1, 0, 1)
            with pool.Fori(1, B // 2) as j:
                for b in range(2):
                    tokens(2 * j + b, j, b)

        @block.scalar
        def _(act):
            def high(dst, src, sem_name):
                nc.scalar.copy(dst, src).then_inc(s[sem_name], 1)

            def shift(i, j, b):
                act.wait_ge(x_in[b], 16 * X_DMAS * (j + 1))
                at_least(act, s["tok_done"], i - 1)
                g = GRID
                nc.scalar.copy(xk[b][:, 6, :, 0:g - 1], xk[b][:, 0, :, 1:g])
                nc.scalar.copy(xk[b][0:64, 7, :, 0:g - 1], xk[b][0:64, 1, :, 1:g])
                nc.scalar.copy(xk[b][64:P, 7, :, 1:g], xk[b][64:P, 4, :, 0:g - 1])
                nc.scalar.copy(xk[b][:, 8, :, 1:g], xk[b][:, 5, :, 0:g - 1]).then_inc(s["x_shift"], 1)

            def attend(i, j, b, first=False, last=False):
                act.wait_ge(s["xn_turned"], i + 1)
                at_least(act, s["v_done"], i)
                high(x_h[:], ps_t[:, 0:2 * N].rearrange("p (a n) -> p a n", a=2), "xh_ready")
                at_least(act, s["aug_stored"], 64 * i)
                act.wait_ge(s["qk_done"], 2 * i + 1)
                high(qk_c[:, 0:2, 0, :], ps_a[0:96, 0:2 * N].rearrange("p (a n) -> p a n", a=2), "qh_ready")
                act.wait_ge(s["qk_done"], 2 * i + 2)
                high(qk_c[:, 2:4, 1, :], ps_b[0:96, 0:2 * N].rearrange("p (a n) -> p a n", a=2), "qh_ready")
                act.wait_ge(s["v_done"], i + 1)
                at_least(act, s["av_done"], i - 1)
                nc.scalar.copy(v[b][:, :, :, 0:HD], ps_t[0:TOK, 0:2 * E].rearrange("p (t h d) -> p t h d", t=2, h=HEADS)
                               ).then_inc(s["v_ready"], 1)
                if not first:
                    outputs(i - 1)
                if not last:
                    shift(i + 2, j + 1, b)
                act.wait_ge(s["max_turned"], i + 1)
                if not first:
                    act.wait_ge(max_in[1 - b], 32 * (j if b == 0 else j + 1))
                nc.scalar.activation(neg_max[:], ps_b[0:HEADS, 0:N], ACT.Copy, scale=-1.0).then_inc(s["max_ready"], 1)
                for g in range(6):
                    act.wait_ge(s["exp_scores"], 6 * i + g + 1)
                    t, pp = g // 3, 2 * (g % 3)
                    nc.scalar.activation(probs[b][:, t, pp:pp + 2], scores(g % 2), ACT.Exp, scale=SCALE
                                         ).then_inc(s["exp_done"], 1)

            def outputs(i):
                act.wait_ge(s["o_turned"], i + 1)
                at_least(act, s["proj_done"], i)
                high(o_h[:], ps_t[:, 0:2 * N].rearrange("p (a n) -> p a n", a=2), "oh_ready")

            shift(0, 0, 0)
            shift(1, 0, 1)
            act.wait_ge(s["w_load"], W_TOTAL)
            high(wqk_h[:], wqk_f[:], "w_split")
            high(wv_h[:], wv_f[:], "w_split")
            high(wp_h[:], wp_f[:], "w_split")

            attend(0, 0, 0, first=True)
            attend(1, 0, 1)
            with act.Fori(1, B // 2 - 1) as j:
                attend(2 * j, j, 0)
                attend(2 * j + 1, j, 1)
            attend(B - 2, B // 2 - 1, 0, last=True)
            attend(B - 1, B // 2 - 1, 1, last=True)
            outputs(B - 1)

        @block.tensor
        def _(pe):
            def contract(out, lhs, rhs):
                for n, (a, c) in enumerate(zip(lhs, rhs)):
                    mm = pe.matmul(out, a, c, start=(n == 0), stop=(n == len(lhs) - 1))
                return mm

            def act_parts(hi, lo, cols):
                return [hi[:, 0, cols], hi[:, 0, cols], lo[:, 0, cols], lo[:, 1, cols], lo[:, 1, cols]]

            def w_parts(hi, lo, cols):
                return [hi[:, 0, cols], lo[:, 0, cols], hi[:, 0, cols], hi[:, 1, cols], lo[:, 1, cols]]

            def project_patches(i, j, b, part):
                if part == 0:
                    pe.wait_ge(x_in[b], 16 * X_DMAS * (j + 1))
                    pe.wait_ge(s["x_shift"], i + 1)
                    at_least(pe, s["tok_biased"], i)
                t, ks = ((0, range(12)), (1, range(6)), (1, range(6, 12)))[part]
                for k in ks:
                    x_tile = xk[b][:, k].rearrange("p a c -> p (a c)")[:, t * PT:(t + 1) * PT]
                    mm = pe.matmul(ps_tok[0:PT, t * E:(t + 1) * E], x_tile, w_tok[:, k, :],
                                   start=(k == 0), stop=(k == KC + KH - 1))
                if part == 2:
                    mm.then_inc(s["tok_done"], 1)

            def turn(src, dst):
                for t in range(2):
                    pe.transpose(dst[:, t * TOK:(t + 1) * TOK], src[:, t, 0:P], ident[0:TOK, 0:TOK])
                    mm = pe.transpose(dst[:, N + t * TOK:N + (t + 1) * TOK],
                                      src[:, t, P:EW],
                                      ident[0:TOK, 0:TOK])
                return mm

            def queries_keys(i, j, b):
                pe.wait_ge(s["xn_ready"], i + 1)
                turn(xn[b], ps_t).then_inc(s["xn_turned"], 1)
                pe.wait_ge(s["xh_ready"], i + 1)
                pe.wait_ge(s["xl_ready"], i + 1)
                at_least(pe, s["h1_ready"], i - 1)
                at_least(pe, s["max_ready"], i)
                everything = slice(0, N)
                for m in range(4):
                    out = (ps_a, ps_b)[m // 2][0:96, (m % 2) * N:(m % 2 + 1) * N]
                    mm = contract(out, w_parts(wqk_h, wqk_l, slice(96 * m, 96 * m + 96)),
                                  act_parts(x_h, x_l, everything))
                    if m % 2:
                        mm.then_inc(s["qk_done"], 1)
                for t in range(2):
                    mm = contract(ps_t[0:TOK, t * E:(t + 1) * E],
                                  act_parts(x_h, x_l, slice(t * TOK, (t + 1) * TOK)),
                                  w_parts(wv_h, wv_l, slice(0, E)))
                mm.then_inc(s["v_done"], 1)

            def max_scores(i, j, b):
                pe.wait_ge(q_in[b], 16 * Q_DMAS * (j + 1))
                for g in range(6):
                    t, pp = g // 3, 2 * (g % 3)
                    if g < 2:
                        at_least(pe, s["exp_done"], 6 * (i - 1) + g + 5)
                    else:
                        pe.wait_ge(s["max_read"], 6 * i + g - 1)
                    for a in range(2):
                        for e in range(2):
                            mm = pe.matmul(ps_s[0:TOK, 2 * (g % 2) + a, e * N:(e + 1) * N],
                                           q_aug[b][:, pp + a, t * TOK:(t + 1) * TOK],
                                           k_aug[b][e][:, pp + a, :], start=True, stop=True)
                    mm.then_inc(s["max_scores"], 1)

            def turn_max(i):
                pe.wait_ge(s["max_read"], 6 * i + 6)
                pe.wait_ge(s["ql_ready"], 2 * i + 2)
                for t in range(2):
                    mm = pe.transpose(ps_b[0:HEADS, t * TOK:(t + 1) * TOK],
                                      maxes[:, t].rearrange("p e a -> p (e a)"), ident[0:TOK, 0:TOK])
                mm.then_inc(s["max_turned"], 1)

            def key_scores(i, j, b):
                pe.wait_ge(max_in[b], 32 * (j + 1))
                for g in range(6):
                    t, pp = g // 3, 2 * (g % 3)
                    if g >= 2:
                        pe.wait_ge(s["exp_done"], 6 * i + g - 1)
                    for a in range(2):
                        for e in range(2):
                            mm = pe.matmul(ps_s[0:TOK, 2 * (g % 2) + a, e * N:(e + 1) * N],
                                           k_aug[b][e][:, pp + a, t * TOK:(t + 1) * TOK],
                                           q_aug[b][:, pp + a, :], start=True, stop=True)
                    mm.then_inc(s["exp_scores"], 1)

            def attend(i, b):
                pe.wait_ge(s["exp_done"], 6 * i + 6)
                pe.wait_ge(s["v_ready"], i + 1)
                w_ = HD + 1
                for t in range(2):
                    for hd in range(HEADS):
                        c = (t * HEADS + hd) * w_
                        for k in range(2):
                            mm = pe.matmul(ps_a[0:TOK, c:c + w_],
                                           probs[b][:, k, hd // 2, hd % 2, t * TOK:(t + 1) * TOK],
                                           v[b][:, k, hd, :], start=(k == 0), stop=(k == 1))
                mm.then_inc(s["av_done"], 1)

            def output(i):
                pe.wait_ge(s["o_ready"], i + 1)
                turn(o_n, ps_t).then_inc(s["o_turned"], 1)
                pe.wait_ge(s["oh_ready"], i + 1)
                pe.wait_ge(s["ol_ready"], i + 1)
                for t in range(2):
                    mm = contract(ps_a[0:TOK, t * E:(t + 1) * E],
                                  act_parts(o_h, o_l, slice(t * TOK, (t + 1) * TOK)),
                                  w_parts(wp_h, wp_l, slice(0, E)))
                mm.then_inc(s["proj_done"], 1)

            def step(i, j, b, first=False, last=False):
                queries_keys(i, j, b)
                if not first:
                    pe.wait_ge(s["ql_ready"], 2 * i + 2)
                    pe.wait_ge(s["qh_ready"], 2 * i + 2)
                    attend(i - 1, 1 - b)
                pe.wait_ge(s["v_ready"], i + 1)
                if not first:
                    output(i - 1)
                if not last:
                    project_patches(i + 1, j + b, 1 - b, 0)
                max_scores(i, j, b)
                if not last:
                    project_patches(i + 1, j + b, 1 - b, 1)
                turn_max(i)
                if not last:
                    project_patches(i + 1, j + b, 1 - b, 2)
                key_scores(i, j, b)

            pe.wait_ge(s["sums"], 4)
            for part in range(3):
                project_patches(0, 0, 0, part)
            pe.wait_ge(s["w_split"], 6)
            step(0, 0, 0, first=True)
            step(1, 0, 1)
            with pe.Fori(1, B // 2 - 1) as j:
                step(2 * j, j, 0)
                step(2 * j + 1, j, 1)
            step(B - 2, B // 2 - 1, 0)
            step(B - 1, B // 2 - 1, 1, last=True)
            attend(B - 1, 1)
            output(B - 1)

        @block.vector
        def _(dve):
            for b in range(2):
                nc.vector.memset(xk[b][:, KC:KC + KH].rearrange("p t a c -> p (t a c)"), 0.0)
                for e in range(2):
                    nc.vector.memset(k_aug[b][e][:].rearrange("p a n -> p (a n)").bitcast(F32), 0.0
                                     ).then_inc(s["const_ready"], 1)
                nc.vector.memset(q_aug[b][:].rearrange("p a n -> p (a n)").bitcast(F32), 0.0)
                nc.vector.memset(v[b][:].rearrange("p t h d -> p (t h d)"), 1.0)
            nc.vector.memset(low_half[0:64, :], 0.0)
            nc.vector.memset(low_half[64:P, :], -1.0)
            nc.vector.memset(eps[:], LN_EPS)
            nc.vector.memset(neg_half[:], -0.5).then_inc(s["zeroed"], 1)

            dve.wait_ge(s["w_load"], W_TOTAL)
            for n in range(4):
                at_least(dve, s["sums"], n)
                nc.vector.tensor_tensor(w_tok[:, 0:KC, :], w_tok[:, 0:KC, :], w_add[:, n], ALU.add
                                        ).then_inc(s["sums"], 1)

            dve.wait_ge(s["w_split"], 3)
            for f, hi, lo in ((wqk_f, wqk_h, wqk_l), (wv_f, wv_h, wv_l), (wp_f, wp_h, wp_l)):
                nc.vector.tensor_tensor(lo[:], f[:], hi[:].bitcast(F32), ALU.subtract).then_inc(s["w_split"], 1)

            def moments(src, rows, k, sem_name):
                for t in range(2):
                    nc.vector.bn_stats(stats[0:rows, k + t, :], src[0:rows, t, :]).then_inc(s["chain"], 1)

            def tokens(i, j, b):
                dve.wait_ge(s["tok_done"], i + 1)
                at_least(dve, s["nrm1"], i)
                nc.vector.tensor_tensor(h_pre[0:PT], ps_tok[0:PT, 0:2 * E].rearrange("p (t e) -> p t e", t=2),
                                        tokb[0:PT].unsqueeze(1).broadcast_to([PT, 2, E]), ALU.add
                                        ).then_inc(s["tok_biased"], 1)
                dve.wait_ge(s["tok_biased"], i + 1)
                moments(h_pre, PT, 0, None)
                dve.wait_ge(s["chain"], 4 * i + 2)
                nc.vector.memset(wait_pad[:, 0:1], 0.0)
                for t in range(2):
                    ins = nc.vector.bn_aggr(mv[0:PT, t, :], stats[0:PT, t, :])
                ins.then_inc(s["stats1"], 1)
                dve.wait_ge(s["rstd1"], i + 1)
                at_least(dve, s["h_ready"], i)
                for t in range(2):
                    ins = nc.vector.tensor_scalar(h_nrm[0:PT, t, :], h_pre[0:PT, t, :], mv[0:PT, t, 0:1],
                                                  rstd[0:PT, t:t + 1], ALU.subtract, ALU.mult)
                ins.then_inc(s["nrm1"], 1)

            def norm2(i, j, b):
                dve.wait_ge(s["h_ready"], i + 1)
                dve.wait_ge(txt_in[b], 16 * (j + 1))
                moments(h[b], TOK, 2, None)
                dve.wait_ge(s["chain"], 4 * i + 4)
                nc.vector.memset(wait_pad[:, 0:1], 0.0)
                for t in range(2):
                    ins = nc.vector.bn_aggr(mv[:, 2 + t, :], stats[:, 2 + t, :])
                ins.then_inc(s["stats2"], 1)
                dve.wait_ge(s["rstd2"], i + 1)
                at_least(dve, s["xn_turned"], i - 1)
                for t in range(2):
                    ins = nc.vector.tensor_scalar(xn[b][:, t, 0:E], h[b][:, t, :], mv[:, 2 + t, 0:1],
                                                  rstd[:, 2 + t:3 + t], ALU.subtract, ALU.mult)
                ins.then_inc(s["xn_once"], 1)
                dve.wait_ge(s["xn_once"], i + 1)
                nc.vector.tensor_copy(xn[b][:, :, E:EW], xn[b][:, :, P:E]).then_inc(s["xn_ready"], 1)

            def low_parts(src, hi, lo, sem_name):
                nc.vector.tensor_tensor(lo[:, 0, :], src[:, 0:N], hi[:, 0, :].bitcast(F32), ALU.subtract)
                nc.vector.scalar_tensor_tensor(lo[:, 1, :], hi[:, 1, :].bitcast(F32), low_half[:, 0:1],
                                               src[:, N:2 * N], ALU.mult, ALU.add).then_inc(s[sem_name], 1)

            def low_qk(i, j, b):
                dve.wait_ge(s["xh_ready"], i + 1)
                at_least(dve, s["v_done"], i)
                low_parts(ps_t, x_h, x_l, "xl_ready")
                for m, (ps, slot) in enumerate(((ps_a, 1), (ps_b, 0))):
                    dve.wait_ge(s["qh_ready"], 2 * i + 1 + m)
                    nc.vector.tensor_tensor(qk_c[:, 2 * m:2 * m + 2, slot, :],
                                            ps[0:96, 0:2 * N].rearrange("p (a n) -> p a n", a=2),
                                            qk_c[:, 2 * m:2 * m + 2, 1 - slot, :].bitcast(F32),
                                            ALU.subtract).then_inc(s["ql_ready"], 1)

            def read_max(i, g):
                dve.wait_ge(s["max_scores"], 6 * i + g + 1)
                if g == 0:
                    at_least(dve, s["max_turned"], i)
                t, pp = g // 3, 2 * (g % 3)
                nc.vector.tensor_reduce(maxes[:, t, :, pp:pp + 2].rearrange("p e a -> p a e"),
                                        scores(g % 2), AX.X, ALU.max).then_inc(s["max_read"], 1)

            def normalise(i):
                dve.wait_ge(s["av_done"], i + 1)
                o = ps_a[0:TOK, 0:2 * HEADS * (HD + 1)].rearrange("p (t h d) -> p t h d", t=2, h=HEADS)
                at_least(dve, s["o_ready"], i)
                nc.vector.reciprocal(r_sum[:], o[:, :, :, HD:HD + 1]).then_inc(s["recip"], 1)
                dve.wait_ge(s["recip"], i + 1)
                at_least(dve, s["o_turned"], i)
                for t in range(2):
                    ins = nc.vector.tensor_tensor(o_n[:, t, 0:E].rearrange("p (h d) -> p h d", h=HEADS), o[:, t, :, 0:HD],
                                                  r_sum[:, t].broadcast_to([TOK, HEADS, HD]), ALU.mult)
                ins.then_inc(s["o_once"], 1)
                dve.wait_ge(s["o_once"], i + 1)
                nc.vector.tensor_copy(o_n[:, :, E:EW], o_n[:, :, P:E]).then_inc(s["o_ready"], 1)

            def low_o(i):
                dve.wait_ge(s["oh_ready"], i + 1)
                at_least(dve, s["proj_done"], i)
                low_parts(ps_t, o_h, o_l, "ol_ready")

            def residual(i, b):
                dve.wait_ge(s["proj_done"], i + 1)
                at_least(dve, h1_out, 16 * i)
                nc.vector.tensor_tensor(h1[:], ps_a[0:TOK, 0:2 * E].rearrange("p (t e) -> p t e", t=2),
                                        h[b][:], ALU.add).then_inc(s["h1_ready"], 1)

            def step(i, j, b, first=False, last=False):
                low_qk(i, j, b)
                if not first:
                    normalise(i - 1)
                    low_o(i - 1)
                    residual(i - 1, 1 - b)
                for g in range(6):
                    read_max(i, g)
                if not last:
                    tokens(i + 1, j + b, 1 - b)
                    norm2(i + 1, j + b, 1 - b)

            tokens(0, 0, 0)
            norm2(0, 0, 0)
            step(0, 0, 0, first=True)
            step(1, 0, 1)
            with dve.Fori(1, B // 2 - 1) as j:
                step(2 * j, j, 0)
                step(2 * j + 1, j, 1)
            step(B - 2, B // 2 - 1, 0)
            step(B - 1, B // 2 - 1, 1, last=True)
            normalise(B - 1)
            low_o(B - 1)
            residual(B - 1, 1)


def stage_experts(nc, B, h1_d, w1, b1, w2, b2, down_w, down_b, up_w, gamma, beta, ident_d, out):
    PAIR = 4
    NN = PAIR * TOK
    steps = B // 2
    with ExitStack() as ctx:
        def sb(name, shape, dt=F32):
            return ctx.enter_context(nc.sbuf_tensor(name, shape, dt))

        def psum(name, shape):
            return ctx.enter_context(nc.psum_tensor(name, shape, F32))

        def sem(name):
            return ctx.enter_context(nc.semaphore(name))

        ident = sb("ident2", [P, P])
        low_half = sb("low_half2", [P, 1])
        neg_half = sb("neg_half2", [P, PAIR])
        eps = sb("eps2", [P, PAIR])
        wait_pad = sb("wait_pad2", [P, 1])
        rank = sb("rank", [P, PAIR, EXPERTS])
        wd_f = sb("wd_f", [P, 2, EXPERTS * DFF])
        wd_h, wd_l = sb("wd_h", [P, 2, EXPERTS * DFF], F32R), sb("wd_l", [P, 2, EXPERTS * DFF], F32R)
        w1_f = sb("w1_f", [P, 2, W1N])
        w1_h, w1_l = sb("w1_h", [P, 2, W1N], F32R), sb("w1_l", [P, 2, W1N], F32R)
        wu = sb("wu", [P, MT, E])
        w2s = sb("w2s", [W1N, EXPERTS])
        b1s = sb("b1s", [W1N, 1])
        b2s = sb("b2s", [P, EXPERTS])
        bd = sb("bd", [P, MT])
        gam = sb("gam", [P, E])
        bet = sb("bet", [P, E])

        hin = [sb(f"hin{b}", [TOK, PAIR, E]) for b in range(2)]
        x2 = [sb(f"x2{b}", [TOK, PAIR, EW]) for b in range(2)]
        x_h = [sb(f"fx_h{b}", [P, 2, NN], F32R) for b in range(2)]
        x_l = [sb(f"fx_l{b}", [P, 2, NN], F32R) for b in range(2)]
        gates = [sb(f"gates{b}", [TOK, PAIR, EXPERTS]) for b in range(2)]
        u = sb("u", [W1N, NN])
        z = [sb(f"z{b}", [P, 2, NN]) for b in range(2)]
        acc = sb("acc", [TOK, PAIR, E])
        y = sb("y", [TOK, PAIR, E])
        y_g = sb("y_g", [TOK, PAIR, E])
        y_b = sb("y_b", [TOK, PAIR, E])
        y_o = sb("y_o", [TOK, PAIR, E])
        stats = sb("fstats", [TOK, 2, PAIR, 6])
        mv = sb("fmv", [TOK, 2, PAIR, 2])
        var_eps = sb("fvar", [TOK, 2, PAIR])
        rstd = sb("frstd", [TOK, 2, PAIR])
        r8 = [sb(f"r8_{n}", [TOK, PAIR, EXPERTS]) for n in range(9)]
        r1 = [sb(f"r1_{n}", [TOK, PAIR, 1]) for n in range(9)]

        ps_d = psum("ps_d", [P, 2, 512])
        ps_u = psum("ps_u", [P, 4, 512])
        ps_x = psum("ps_x", [P, 2, 512])

        names = """w_load consts w_split w_low ln_stats ln_root x_once x_ready turned xh_ready xl_ready
            w1_done u_ready logits_done route_in route_exp route_chain gates_ready
            down_done z_ready up_done acc_done acc_chain y_stats y_root y_ready y_chain out_ready
            ln_chain ln_pool""".split()
        s = {n: sem("f_" + n) for n in names}
        h_in = [sem(f"f_h_in{b}") for b in range(2)]
        stored = sem("f_stored")
        LOADS = 14 * 16
        ROUTE = 21

        block = ctx.enter_context(nc.Block())

        @block.sync
        def _(sp):
            def load(j, jj, b):
                at_least(sp, s["out_ready"], j - 1)
                for a in range(2):
                    sp.dma_start(hin[b][:, 2 * a:2 * a + 2, :], h1_d[2 * j + a]).then_inc(h_in[b], 16)

            load(0, 0, 0)
            loads = [(ident[:, :], ident_d), (wu[:], up_w.rearrange("(m p) e -> p m e", p=P)),
                     (w2s[:, :], w2), (b1s[:, :], b1), (b2s[:, :], b2), (bd[:, :], down_b),
                     (gam[:, :], gamma), (bet[:, :], beta)]
            for f, src in ((w1_f, w1), (wd_f, down_w)):
                loads += [(f[:, 0, :], src[0:P, :]), (f[0:64, 1, :], src[P:E, :]), (f[64:P, 1, :], src[P:E, :])]
            assert 16 * len(loads) == LOADS
            for dst, src in loads:
                sp.dma_start(dst, src).then_inc(s["w_load"], 16)
            load(1, 0, 1)

            def store(j):
                sp.wait_ge(s["out_ready"], j + 1)
                for a in range(2):
                    t = slice(2 * a, 2 * a + 2)
                    sp.dma_start(out[2 * j + a, 0:NP].rearrange("(t p) e -> p t e", p=PT),
                                 y_o[0:PT, t, :]).then_inc(stored, 16)
                    sp.dma_start(out[2 * j + a, NP:N].rearrange("(t p) e -> p t e", p=TT),
                                 y_o[PT:TOK, t, :]).then_inc(stored, 16)

            store(0)
            load(2, 1, 0)
            store(1)
            load(3, 1, 1)
            with sp.Fori(1, steps // 2 - 1) as jj:
                for b in range(2):
                    store(2 * jj + b)
                    load(2 * jj + b + 2, jj + 1, b)
            store(steps - 2)
            store(steps - 1)
            sp.wait_ge(stored, 64 * steps)

        @block.gpsimd
        def _(pool):
            def root(j, n, src, dst):
                pool.wait_ge(s[src], j + 1)
                nc.gpsimd.tensor_tensor(var_eps[:, n], mv[:, n, :, 1], eps[0:TOK, :], ALU.add
                                        ).then_inc(s["ln_pool"], 1)

            def ln_root(j):
                root(j, 0, "ln_stats", "ln_root")
                pool.wait_ge(s["ln_pool"], 2 * j + 1 if isinstance(j, int) and j == 0 else 2 * j)
                nc.gpsimd.tensor_tensor(rstd[:, 0], var_eps[:, 0], neg_half[0:TOK, :], ALU.pow
                                        ).then_inc(s["ln_root"], 1)

            def finish(j, b):
                root(j, 1, "y_stats", "y_root")
                pool.wait_ge(s["ln_pool"], 2 * j + 3)
                nc.gpsimd.tensor_tensor(rstd[:, 1], var_eps[:, 1], neg_half[0:TOK, :], ALU.pow
                                        ).then_inc(s["y_root"], 1)
                pool.wait_ge(s["y_ready"], j + 1)
                nc.gpsimd.tensor_tensor(y_g[:], y[:], gam[0:TOK].unsqueeze(1).broadcast_to([TOK, PAIR, E]),
                                        ALU.mult).then_inc(s["y_chain"], 1)
                pool.wait_ge(s["y_chain"], 2 * j + 1)
                nc.gpsimd.tensor_tensor(y_b[:], y_g[:], bet[0:TOK].unsqueeze(1).broadcast_to([TOK, PAIR, E]),
                                        ALU.add).then_inc(s["y_chain"], 1)
                pool.wait_ge(s["y_chain"], 2 * j + 2)
                at_least(pool, stored, 64 * j)
                nc.gpsimd.tensor_tensor(y_o[:], y_b[:], hin[b][:], ALU.add).then_inc(s["out_ready"], 1)

            pool.wait_ge(s["w_load"], LOADS)
            pool.wait_ge(s["consts"], 1)

            def ln_root_next(j):
                root(j, 0, "ln_stats", "ln_root")
                pool.wait_ge(s["ln_pool"], 2 * j)
                nc.gpsimd.tensor_tensor(rstd[:, 0], var_eps[:, 0], neg_half[0:TOK, :], ALU.pow
                                        ).then_inc(s["ln_root"], 1)

            root(0, 0, "ln_stats", "ln_root")
            pool.wait_ge(s["ln_pool"], 1)
            nc.gpsimd.tensor_tensor(rstd[:, 0], var_eps[:, 0], neg_half[0:TOK, :], ALU.pow
                                    ).then_inc(s["ln_root"], 1)
            for j in range(2):
                ln_root_next(j + 1)
                finish(j, j)
            with pool.Fori(1, steps // 2 - 1) as jj:
                for b in range(2):
                    ln_root_next(2 * jj + b + 1)
                    finish(2 * jj + b, b)
            ln_root_next(steps - 1)
            finish(steps - 2, 0)
            pool.wait_ge(s["y_stats"], steps)
            nc.gpsimd.tensor_tensor(var_eps[:, 1], mv[:, 1, :, 1], eps[0:TOK, :], ALU.add
                                    ).then_inc(s["ln_pool"], 1)
            pool.wait_ge(s["ln_pool"], 2 * steps)
            nc.gpsimd.tensor_tensor(rstd[:, 1], var_eps[:, 1], neg_half[0:TOK, :], ALU.pow
                                    ).then_inc(s["y_root"], 1)
            pool.wait_ge(s["y_ready"], steps)
            nc.gpsimd.tensor_tensor(y_g[:], y[:], gam[0:TOK].unsqueeze(1).broadcast_to([TOK, PAIR, E]),
                                    ALU.mult).then_inc(s["y_chain"], 1)
            pool.wait_ge(s["y_chain"], 2 * steps - 1)
            nc.gpsimd.tensor_tensor(y_b[:], y_g[:], bet[0:TOK].unsqueeze(1).broadcast_to([TOK, PAIR, E]),
                                    ALU.add).then_inc(s["y_chain"], 1)
            pool.wait_ge(s["y_chain"], 2 * steps)
            pool.wait_ge(stored, 64 * (steps - 1))
            nc.gpsimd.tensor_tensor(y_o[:], y_b[:], hin[1][:], ALU.add).then_inc(s["out_ready"], 1)

        @block.scalar
        def _(act):
            act.wait_ge(s["w_load"], LOADS)
            nc.scalar.copy(w1_h[:], w1_f[:]).then_inc(s["w_split"], 1)
            nc.scalar.copy(wd_h[:], wd_f[:]).then_inc(s["w_split"], 1)

            def high_x(j, b):
                act.wait_ge(s["turned"], j + 1)
                at_least(act, s["down_done"], 16 * (j - 1))
                nc.scalar.copy(x_h[b][:], ps_x[:, :, 0:NN]).then_inc(s["xh_ready"], 1)

            def hidden_router(j):
                act.wait_ge(s["w1_done"], j + 1)
                at_least(act, s["logits_done"], j)
                nc.scalar.activation(u[:, :], ps_x[0:W1N, 0, 0:NN], ACT.Gelu, bias=b1s[:, 0:1]
                                     ).then_inc(s["u_ready"], 1)

            def exp_router(j):
                act.wait_ge(s["route_in"], j + 1)
                nc.scalar.activation(r8[2][:], r8[1][:], ACT.Exp).then_inc(s["route_exp"], 1)

            def hidden(j, e):
                at_least(act, s["up_done"], 8 * j + e - 1)
                for n in range(2):
                    m = 2 * e + n
                    act.wait_ge(s["down_done"], 16 * j + m + 1)
                    nc.scalar.activation(z[e % 2][:, n, :], ps_d[:, n, 0:NN], ACT.Gelu, bias=bd[:, m:m + 1]
                                         ).then_inc(s["z_ready"], 1)

            def step(j, b, last=False):
                for e in range(EXPERTS):
                    hidden(j, e)
                    if not last and e == 2:
                        high_x(j + 1, 1 - b)
                    if not last and e == 4:
                        hidden_router(j + 1)
                if not last:
                    exp_router(j + 1)

            high_x(0, 0)
            hidden_router(0)
            exp_router(0)
            step(0, 0)
            step(1, 1)
            with act.Fori(1, steps // 2 - 1) as jj:
                step(2 * jj, 0)
                step(2 * jj + 1, 1)
            step(steps - 2, 0)
            step(steps - 1, 1, last=True)

        @block.tensor
        def _(pe):
            def contract(out_, lhs, rhs):
                for n, (a, c) in enumerate(zip(lhs, rhs)):
                    mm = pe.matmul(out_, a, c, start=(n == 0), stop=(n == len(lhs) - 1))
                return mm

            def x_parts(b):
                hi, lo = x_h[b], x_l[b]
                return [hi[:, 0, :], hi[:, 0, :], lo[:, 0, :], lo[:, 1, :], lo[:, 1, :]]

            def w_parts(hi, lo, cols):
                return [hi[:, 0, cols], lo[:, 0, cols], hi[:, 0, cols], hi[:, 1, cols], lo[:, 1, cols]]

            def turn(j, b):
                pe.wait_ge(s["x_ready"], j + 1)
                at_least(pe, s["route_in"], j)
                for t in range(PAIR):
                    pe.transpose(ps_x[:, 0, t * TOK:(t + 1) * TOK], x2[b][:, t, 0:P], ident[0:TOK, 0:TOK])
                    mm = pe.transpose(ps_x[:, 1, t * TOK:(t + 1) * TOK],
                                      x2[b][:, t, P:EW],
                                      ident[0:TOK, 0:TOK])
                mm.then_inc(s["turned"], 1)

            def router_hidden(j, b):
                pe.wait_ge(s["xh_ready"], j + 1)
                pe.wait_ge(s["xl_ready"], j + 1)
                contract(ps_x[0:W1N, 0, 0:NN], w_parts(w1_h, w1_l, slice(0, W1N)), x_parts(b)
                         ).then_inc(s["w1_done"], 1)

            def logits(j):
                pe.wait_ge(s["u_ready"], j + 1)
                for t in range(PAIR):
                    mm = pe.matmul(ps_x[0:TOK, 1, t * EXPERTS:(t + 1) * EXPERTS], u[:, t * TOK:(t + 1) * TOK],
                                   w2s[:, :], start=True, stop=True)
                mm.then_inc(s["logits_done"], 1)

            def down(j, b, e):
                for n in range(2):
                    m = 2 * e + n
                    at_least(pe, s["z_ready"], 16 * j + m - 1)
                    contract(ps_d[:, n, 0:NN], w_parts(wd_h, wd_l, slice(m * P, (m + 1) * P)), x_parts(b)
                             ).then_inc(s["down_done"], 1)

            def up(j, e):
                pe.wait_ge(s["z_ready"], 16 * j + 2 * e + 2)
                at_least(pe, s["acc_done"], 8 * j + e - 1)
                for t in range(PAIR):
                    for n in range(2):
                        mm = pe.matmul(ps_u[0:TOK, 2 * (e % 2) + t // 2, (t % 2) * E:(t % 2 + 1) * E],
                                       z[e % 2][:, n, t * TOK:(t + 1) * TOK], wu[:, 2 * e + n, :],
                                       start=(n == 0), stop=(n == 1))
                mm.then_inc(s["up_done"], 1)

            def step(j, b, last=False):
                for e in range(EXPERTS):
                    down(j, b, e)
                    if e:
                        up(j, e - 1)
                    if not last and e == 2:
                        turn(j + 1, 1 - b)
                    if not last and e == 4:
                        router_hidden(j + 1, 1 - b)
                    if not last and e == 6:
                        logits(j + 1)
                up(j, EXPERTS - 1)

            pe.wait_ge(s["w_load"], LOADS)
            turn(0, 0)
            pe.wait_ge(s["w_low"], 2)
            router_hidden(0, 0)
            logits(0)
            step(0, 0)
            step(1, 1)
            with pe.Fori(1, steps // 2 - 1) as jj:
                step(2 * jj, 0)
                step(2 * jj + 1, 1)
            step(steps - 2, 0)
            step(steps - 1, 1, last=True)

        @block.vector
        def _(dve):
            nc.vector.memset(low_half[0:64, :], 0.0)
            nc.vector.memset(low_half[64:P, :], -1.0)
            for e in range(EXPERTS):
                nc.vector.memset(rank[:, :, e:e + 1], float(EXPERTS - e))
            nc.vector.memset(eps[:], LN_EPS)
            nc.vector.memset(neg_half[:], -0.5).then_inc(s["consts"], 1)

            def moments(j, n, src, count, sem_name):
                for t in range(PAIR):
                    nc.vector.bn_stats(stats[:, n, t, :], src[:, t, :]).then_inc(s["ln_chain"], 1)
                dve.wait_ge(s["ln_chain"], count)
                nc.vector.memset(wait_pad[:, 0:1], 0.0)
                for t in range(PAIR):
                    ins = nc.vector.bn_aggr(mv[:, n, t, :], stats[:, n, t, :])
                ins.then_inc(s[sem_name], 1)

            def scale(dst, src, n):
                for t in range(PAIR):
                    ins = nc.vector.tensor_scalar(dst[:, t, 0:E], src[:, t, :], mv[:, n, t, 0:1],
                                                  rstd[:, n, t:t + 1], ALU.subtract, ALU.mult)
                return ins

            def norm(j, jj, b):
                dve.wait_ge(h_in[b], 32 * (jj + 1))
                moments(j, 0, hin[b], PAIR if isinstance(j, int) and j == 0 else 8 * j, "ln_stats")
                dve.wait_ge(s["ln_root"], j + 1)
                at_least(dve, s["turned"], j - 1)
                scale(x2[b], hin[b], 0).then_inc(s["x_once"], 1)
                dve.wait_ge(s["x_once"], j + 1)
                nc.vector.tensor_copy(x2[b][:, :, E:EW], x2[b][:, :, P:E]).then_inc(s["x_ready"], 1)

            def low_x(j, b):
                dve.wait_ge(s["xh_ready"], j + 1)
                nc.vector.tensor_tensor(x_l[b][:, 0, :], ps_x[:, 0, 0:NN], x_h[b][:, 0, :].bitcast(F32),
                                        ALU.subtract)
                nc.vector.scalar_tensor_tensor(x_l[b][:, 1, :], x_h[b][:, 1, :].bitcast(F32), low_half[:, 0:1],
                                               ps_x[:, 1, 0:NN], ALU.mult, ALU.add).then_inc(s["xl_ready"], 1)

            def logits_in(j):
                dve.wait_ge(s["logits_done"], j + 1)
                count = ROUTE * j

                nc.vector.tensor_tensor(r8[0][:], ps_x[0:TOK, 1, 0:PAIR * EXPERTS].rearrange(
                    "p (t e) -> p t e", t=PAIR), b2s[0:TOK].unsqueeze(1).broadcast_to([TOK, PAIR, EXPERTS]),
                    ALU.add).then_inc(s["route_chain"], 1)
                dve.wait_ge(s["route_chain"], count + 1)
                nc.vector.tensor_reduce(r1[0][:, :, 0], r8[0][:], AX.X, ALU.max).then_inc(s["route_chain"], 1)
                dve.wait_ge(s["route_chain"], count + 2)
                nc.vector.tensor_tensor(r8[1][:], r8[0][:], wide(r1[0]), ALU.subtract).then_inc(s["route_in"], 1)

            def wide(a):
                return a[:].broadcast_to([TOK, PAIR, EXPERTS])

            def route(j, b):
                dve.wait_ge(s["route_exp"], j + 1)
                at_least(dve, s["acc_done"], 8 * (j - 1))
                n = [ROUTE * j + 2]
                tt, red = nc.vector.tensor_tensor, nc.vector.tensor_reduce

                def link(ins):
                    n[0] = n[0] + 1
                    ins.then_inc(s["route_chain"], 1)
                    dve.wait_ge(s["route_chain"], n[0])

                link(red(r1[1][:, :, 0], r8[2][:], AX.X, ALU.add))
                link(nc.vector.reciprocal(r1[2][:], r1[1][:]))
                link(tt(r8[3][:], r8[2][:], wide(r1[2]), ALU.mult))
                link(red(r1[3][:, :, 0], r8[3][:], AX.X, ALU.max))
                link(tt(r8[4][:], r8[3][:], wide(r1[3]), ALU.is_ge))
                link(tt(r8[5][:], r8[4][:], rank[0:TOK], ALU.mult))
                link(red(r1[4][:, :, 0], r8[5][:], AX.X, ALU.max))
                link(tt(r8[4][:], r8[5][:], wide(r1[4]), ALU.is_ge))
                link(nc.vector.scalar_tensor_tensor(r8[6][:], r8[4][:], -2.0, r8[3][:], ALU.mult, ALU.add))
                link(red(r1[5][:, :, 0], r8[6][:], AX.X, ALU.max))
                link(tt(r8[5][:], r8[6][:], wide(r1[5]), ALU.is_ge))
                link(tt(r8[7][:], r8[5][:], rank[0:TOK], ALU.mult))
                link(red(r1[6][:, :, 0], r8[7][:], AX.X, ALU.max))
                link(tt(r8[5][:], r8[7][:], wide(r1[6]), ALU.is_ge))
                link(tt(r8[6][:], r8[4][:], r8[5][:], ALU.add))
                link(tt(r8[8][:], r8[6][:], r8[3][:], ALU.mult))
                link(red(r1[7][:, :, 0], r8[8][:], AX.X, ALU.add))
                link(nc.vector.tensor_scalar(r1[8][:], r1[7][:], GATE_EPS, None, ALU.add))
                link(nc.vector.reciprocal(r1[2][:], r1[8][:]))
                tt(gates[b][:], r8[8][:], wide(r1[2]), ALU.mult).then_inc(s["gates_ready"], 1)

            def gather(j, b, e):
                dve.wait_ge(s["up_done"], 8 * j + e + 1)
                if e == 0:
                    dve.wait_ge(s["gates_ready"], j + 1)
                    at_least(dve, s["y_ready"], j)
                else:
                    dve.wait_ge(s["acc_done"], 8 * j + e)
                for t in range(PAIR):
                    base = x2[b] if e == 0 else acc
                    ins = nc.vector.scalar_tensor_tensor(
                        acc[:, t, :], ps_u[0:TOK, 2 * (e % 2) + t // 2, (t % 2) * E:(t % 2 + 1) * E],
                        gates[b][:, t, e:e + 1], base[:, t, 0:E], ALU.mult, ALU.add)
                ins.then_inc(s["acc_done"], 1)

            def result(j, b, last=False):
                dve.wait_ge(s["acc_done"], 8 * j + 8)
                moments(j, 1, acc, 8 * j + (8 if last else 12), "y_stats")
                dve.wait_ge(s["y_root"], j + 1)
                at_least(dve, s["y_chain"], 2 * j)
                scale(y, acc, 1).then_inc(s["y_ready"], 1)

            def step(j, jj, b, last=False):
                for e in range(EXPERTS):
                    if not last:
                        if e == 0:
                            norm(j + 1, jj + b, 1 - b)
                        if e == 2:
                            low_x(j + 1, 1 - b)
                        if e == 6:
                            logits_in(j + 1)
                    gather(j, b, e)
                if not last:
                    route(j + 1, 1 - b)
                result(j, b, last)

            norm(0, 0, 0)
            dve.wait_ge(s["w_split"], 2)
            for f, hi, lo in ((w1_f, w1_h, w1_l), (wd_f, wd_h, wd_l)):
                nc.vector.tensor_tensor(lo[:], f[:], hi[:].bitcast(F32), ALU.subtract).then_inc(s["w_low"], 1)
            low_x(0, 0)
            logits_in(0)
            route(0, 0)
            step(0, 0, 0)
            step(1, 0, 1)
            with dve.Fori(1, steps // 2 - 1) as jj:
                step(2 * jj, jj, 0)
                step(2 * jj + 1, jj, 1)
            step(steps - 2, steps // 2 - 1, 0)
            step(steps - 1, steps // 2 - 1, 1, last=True)


def early_fusion(nc, x_k, txt, w_center, w_halo, tok_b, tok_g, tok_beta, wqk, wv, wproj,
                 w1, b1, w2, b2, down_w, down_b, up_w, gamma, beta, ident, out):
    B = x_k.shape[0]
    aug_d = nc.dram_tensor("aug_d", (2, 4, 34, PAIRS, N), F32, kind="Internal").ap()
    h1_d = nc.dram_tensor("h1_d", (B, TOK, 2, E), F32, kind="Internal").ap()
    stage_attention(nc, B, x_k, txt, w_center, w_halo, tok_b, tok_g, tok_beta, wqk, wv, wproj, ident, aug_d, h1_d)
    stage_experts(nc, B, h1_d, w1, b1, w2, b2, down_w, down_b, up_w, gamma, beta, ident, out)


def kernel(**inputs):
    import numpy as np
    import concourse.bacc as bacc
    from concourse.bass_utils import run_bass_kernel_spmd

    a = {k.removeprefix("L0_"): np.asarray(v) for k, v in inputs.items()}
    B = a["x"].shape[0]
    rows = KC * P
    x_k = a["x"].reshape(B, 3, GRID, 16, GRID, 16).transpose(0, 5, 1, 3, 2, 4).reshape(B, rows, NP)
    w5 = a["tok_proj_w"].reshape(E, 16, 16, 5, 3).transpose(3, 2, 4, 1, 0)
    center = np.zeros_like(w5)
    center[0] = w5[0]
    center[1][:12] = w5[1][4:]
    center[2][:, :, :12] = w5[2][:, :, 4:]
    center[3][4:] = w5[3][:12]
    center[4][:, :, 4:] = w5[4][:, :, :12]
    right, left = w5[3].reshape(rows, E), w5[1].reshape(rows, E)
    halo = np.concatenate([right[576:768], left[0:192],
                           w5[2][:, :, 0:4].reshape(192, E), w5[4][:, :, 12:16].reshape(192, E)])
    wq = a["attn_Wq"].reshape(PAIRS, 2, HD, E).transpose(1, 2, 0, 3)
    wkv = a["attn_Wkv"].reshape(HEADS, 2, HD, E)
    wk = wkv[:, 0].reshape(PAIRS, 2, HD, E).transpose(1, 2, 0, 3)
    wqk = np.concatenate([wq.reshape(E, E), wk.reshape(E, E)]).T
    wide = lambda v: np.broadcast_to(v, (P, v.shape[-1]))
    named = {
        "x_k": x_k, "txt": a["txt"], "w_center": center.reshape(5, rows, E), "w_halo": halo,
        "tok_b": wide(a["tok_proj_b"]), "tok_g": wide(a["tok_gamma"]), "tok_beta": wide(a["tok_beta"]),
        "wqk": wqk, "wv": wkv[:, 1].reshape(E, E).T, "wproj": a["attn_Wproj"].T,
        "w1": a["ffn_w1"], "b1": a["ffn_b1"].reshape(W1N, 1), "w2": a["ffn_w2"], "b2": wide(a["ffn_b2"]),
        "down_w": a["ffn_down_w"].transpose(1, 0, 2).reshape(E, EXPERTS * DFF),
        "down_b": a["ffn_down_b"].reshape(MT, P).T, "up_w": a["ffn_up_w"].reshape(EXPERTS * DFF, E),
        "gamma": wide(a["ffn_gamma"]), "beta": wide(a["ffn_beta"]), "ident": np.eye(P, dtype=np.float32),
    }
    nc = bacc.Bacc("TRN2", target_bir_lowering=False, num_devices=1)
    arrays, args = {}, []
    for name, value in named.items():
        arrays[f"in_{name}"] = np.ascontiguousarray(value)
        args.append(nc.dram_tensor(f"in_{name}", value.shape, F32, kind="ExternalInput").ap())
    args.append(nc.dram_tensor("out", (B, N, E), F32, kind="ExternalOutput").ap())
    early_fusion(nc, *args)
    return run_bass_kernel_spmd(nc, [arrays], core_ids=[0]).results[0]["out"]
```

```python
from contextlib import ExitStack

from concourse import mybir

ALU = mybir.AluOpType
ACT = mybir.ActivationFunctionType
AX = mybir.AxisListType
F32 = mybir.dt.float32
F32R = mybir.dt.float32r

P = 128
E = 192
EW = 256
HEADS, HD = 12, 16
PAIRS = HEADS // 2
GRID = 14
NP = GRID * GRID
TXT = 32
PT, TT = NP // 2, TXT // 2
TOK = PT + TT
N = 2 * TOK
KC, KH = 6, 6
LN_EPS = 1e-5
GATE_EPS = 1e-8
SCALE = HD ** -0.5
MASKED = -(2.0 ** 100)
EXPERTS, DFF = 8, 256
MT = EXPERTS * DFF // P
W1N = E // 2


def at_least(eng, sem, count):
    if not isinstance(count, int) or count > 0:
        eng.wait_ge(sem, count)


class Image:

    def __init__(self, jj, k, B):
        self.n = 4 * jj + k
        self.half = 2 * jj + k // 2
        self.par, self.quad = k % 2, k % 4
        self.live = not isinstance(self.n, int) or 0 <= self.n < B


def run_steps(eng, B, step):
    def peeled(i):
        step(lambda d: Image(0, i + d, B))

    for i in range(4):
        peeled(i)
    with eng.Fori(1, B // 4 - 1) as jj:
        for q in range(4):
            step(lambda d: Image(jj, q + d, B))
    for i in range(B - 4, B + 2):
        peeled(i)


def stage_attention(nc, B, x_k, txt, w_center, w_halo, tok_b, tok_g, tok_beta, wqk, wv, wproj,
                    ident_d, aug_d, h1_d):
    with ExitStack() as ctx:
        def sb(name, shape, dt=F32):
            return ctx.enter_context(nc.sbuf_tensor(name, shape, dt))

        def psum(name, shape):
            return ctx.enter_context(nc.psum_tensor(name, shape, F32))

        def sem(name):
            return ctx.enter_context(nc.semaphore(name))

        ident = sb("ident", [P, P])
        low_half = sb("low_half", [P, 1])
        neg_half = sb("neg_half", [P, 2])
        eps = sb("eps", [P, 2])
        wait_pad = sb("wait_pad", [P, 1])
        w_tok = sb("w_tok", [P, KC + KH, E])
        w_add = sb("w_add", [P, 4, KC, E])
        tokb = sb("tokb", [P, E])
        tokg = sb("tokg", [P, E])
        tokbeta = sb("tokbeta", [P, E])
        wqk_f = sb("wqk_f", [P, 2, 2 * E])
        wv_f = sb("wv_f", [P, 2, E])
        wp_f = sb("wp_f", [P, 2, E])
        wqk_h, wqk_l = sb("wqk_h", [P, 2, 2 * E], F32R), sb("wqk_l", [P, 2, 2 * E], F32R)
        wv_h, wv_l = sb("wv_h", [P, 2, E], F32R), sb("wv_l", [P, 2, E], F32R)
        wp_h, wp_l = sb("wp_h", [P, 2, E], F32R), sb("wp_l", [P, 2, E], F32R)
        key_rows = sb("key_rows", [1, 2, PAIRS, N])
        query_rows = sb("query_rows", [PAIRS, 2, N])

        xk = [sb(f"xk{b}", [P, KC + KH, GRID, GRID]) for b in range(2)]
        h = [sb(f"tok{b}", [TOK, 2, E]) for b in range(4)]
        xn = [sb(f"xn{b}", [TOK, 2, EW]) for b in range(2)]
        v = [sb(f"v{b}", [TOK, 2, HEADS, 32]) for b in range(2)]
        q_aug = [sb(f"q_aug{b}", [P, PAIRS, N], F32R) for b in range(2)]
        k_aug = [[sb(f"k_aug{b}{e}", [P, PAIRS, N], F32R) for e in range(2)] for b in range(2)]
        probs = sb("probs", [TOK, 2, PAIRS, 2, N])
        h_pre = sb("h_pre", [TOK, 2, E])
        h_gam = sb("h_gam", [TOK, 2, E])
        stats = sb("stats", [TOK, 4, 6])
        mv = sb("mv", [TOK, 4, 2])
        var_eps = sb("var_eps", [TOK, 4])
        rstd = sb("rstd", [TOK, 4])
        x_h, x_l = sb("x_h", [P, 2, N], F32R), sb("x_l", [P, 2, N], F32R)
        o_h, o_l = sb("o_h", [P, 2, N], F32R), sb("o_l", [P, 2, N], F32R)
        qk_c = sb("qk_c", [96, 4, 2, N], F32R)
        maxes = sb("maxes", [TOK, 2, 2, PAIRS])
        neg_max = sb("neg_max", [HEADS, N], F32R)
        o_t = sb("o_t", [P, 3, N])
        o_n = sb("o_n", [TOK, 2, EW])
        r_sum = sb("r_sum", [TOK, 2, HEADS, 1])
        h1 = sb("h1", [TOK, 2, E])

        ps_s = psum("ps_s", [P, 4, 512])
        ps_tok = psum("ps_tok", [P, 512])
        ps_t = psum("ps_t", [P, 512])
        ps_a = psum("ps_a", [P, 512])
        ps_b = psum("ps_b", [P, 512])

        names = """w_load const_ready w_split
            x_shift tok_done tok_biased stats1 rstd1 centred h_ready stats2 rstd2 xn_once xn_ready
            xn_turned xh_ready xl_ready qk_done qh_ready ql_ready v_done v_ready
            aug_stored max_scores max_read max_turned max_ready exp_scores exp_done
            av_done ot_ready o_tokens recip o_once o_ready o_turned oh_ready ol_ready proj_done h1_ready sums chain zeroed
            const_chain ln_chain""".split()
        s = {n: sem(n) for n in names}
        x_in = [sem(f"x_in{b}") for b in range(2)]
        txt_in = [sem(f"txt_in{b}") for b in range(2)]
        q_in = [sem(f"q_in{b}") for b in range(2)]
        max_in = [sem(f"max_in{b}") for b in range(2)]
        h1_out = sem("h1_out")

        X_DMAS, Q_DMAS = 5, 8

        def scores(b):
            return ps_s[0:TOK, 2 * b:2 * b + 2, 0:2 * N].rearrange("p a (e n) -> p a e n", e=2)

        block = ctx.enter_context(nc.Block())

        @block.sync
        def _(sp):
            def w(dst, src):
                sp.dma_start(dst, src).then_inc(s["w_load"], 16)

            w(ident[:, :], ident_d)
            w(w_tok[:, 0:KC, :], w_center[0].rearrange("(t p) e -> p t e", p=P))
            for i in range(4):
                w(w_add[:, i, :, :], w_center[i + 1].rearrange("(t p) e -> p t e", p=P))
            w(w_tok[:, KC:KC + KH, :], w_halo.rearrange("(t p) e -> p t e", p=P))
            w(tokb[:, :], tok_b)
            w(tokg[:, :], tok_g)
            w(tokbeta[:, :], tok_beta)
            for dst, src in ((wqk_f, wqk), (wv_f, wv), (wp_f, wproj)):
                w(dst[:, 0, :], src[0:P, :])
                w(dst[0:64, 1, :], src[P:E, :])
                w(dst[64:P, 1, :], src[P:E, :])

            sp.wait_ge(s["const_ready"], 8)
            for e in range(2):
                for c in range(2):
                    row = 32 + c
                    sp.dma_start(aug_d[0, e, row],
                                 query_rows[:, c, :]).then_inc(s["w_load"], 16)
                    sp.dma_start(aug_d[1, e, row],
                                 query_rows[:, c, :]).then_inc(s["w_load"], 16)

            def load_image(im):
                i, b = im.n, im.par
                at_least(sp, s["tok_done"], i - 1)
                src = x_k[i]
                sp.dma_start(xk[b][:, 0:KC].rearrange("p t a c -> p t (a c)"),
                             src.rearrange("(t p) g -> p t g", p=P)).then_inc(x_in[b], 16)
                rows = src.rearrange("(cc r) g -> cc r g", r=16)
                cut = NP - GRID
                sp.dma_start(xk[b][:, 9, 1:GRID, :], rows[0:32, 12:16, 0:cut]).then_inc(x_in[b], 16)
                sp.dma_start(xk[b][0:64, 10, 1:GRID, :], rows[32:48, 12:16, 0:cut]).then_inc(x_in[b], 16)
                sp.dma_start(xk[b][64:P, 10, 0:GRID - 1, :], rows[0:16, 0:4, GRID:NP]).then_inc(x_in[b], 16)
                sp.dma_start(xk[b][:, 11, 0:GRID - 1, :], rows[16:48, 0:4, GRID:NP]).then_inc(x_in[b], 16)

            def load_text(im):
                at_least(sp, s["h1_ready"], im.n - 3)
                sp.dma_start(h[im.quad][PT:TOK, :, :], txt[im.n].rearrange("(t p) e -> p t e", p=TT)
                             ).then_inc(txt_in[im.par], 16)

            def store_qk(im):
                i, b = im.n, im.par
                sp.wait_ge(s["qh_ready"], 2 * i + 2)
                sp.wait_ge(s["ql_ready"], 2 * i + 2)
                for t in range(4):
                    sp.dma_start(aug_d[b, t, 0:32].rearrange("(l d) p n -> (d p) l n", l=2),
                                 qk_c[:, t].bitcast(F32)).then_inc(s["aug_stored"], 16)

            def load_qk(im):
                b = im.par
                sp.wait_ge(s["aug_stored"], 64 * (im.n + 1))
                for e in range(2):
                    r = 64 * e
                    sp.dma_start(q_aug[b][r:r + 16].bitcast(F32), aug_d[b, e, 0:16]).then_inc(q_in[b], 16)
                    sp.dma_start(q_aug[b][r + 16:r + 50].bitcast(F32), aug_d[b, e, 0:34]).then_inc(q_in[b], 16)
                    sp.dma_start(k_aug[b][e][r:r + 16].bitcast(F32), aug_d[b, 2 + e, 16:32]).then_inc(q_in[b], 16)
                    sp.dma_start(k_aug[b][e][r + 16:r + 48].bitcast(F32), aug_d[b, 2 + e, 0:32]).then_inc(q_in[b], 16)

            def place_max(im):
                b = im.par
                sp.wait_ge(s["max_ready"], im.n + 1)
                for e in range(2):
                    sp.dma_start(q_aug[b][64 * e + 49:64 * e + 50].bitcast(F32), neg_max[e * PAIRS:(e + 1) * PAIRS, :].bitcast(F32)
                                 ).then_inc(max_in[b], 16)

            def store_h1(im):
                sp.wait_ge(s["h1_ready"], im.n + 1)
                sp.dma_start(h1_d[im.n], h1[:, :, :]).then_inc(h1_out, 16)

            sp.wait_ge(s["const_ready"], 8)
            for b in range(2):
                for e in range(2):
                    r = 64 * e + 48
                    for c in range(2):
                        sp.dma_start(k_aug[b][e][r + c:r + c + 1].bitcast(F32),
                                     key_rows[:, c]).then_inc(s["w_load"], 16)
            sp.wait_ge(s["zeroed"], 1)
            load_image(Image(0, 0, B))
            load_text(Image(0, 0, B))
            load_image(Image(0, 1, B))

            def step(at):
                if at(2).live:
                    load_image(at(2))
                if at(1).live:
                    load_text(at(1))
                if at(0).live:
                    store_qk(at(0))
                if at(-1).live:
                    place_max(at(-1))
                if at(0).live:
                    load_qk(at(0))
                if at(-2).live:
                    store_h1(at(-2))

            run_steps(sp, B, step)
            sp.wait_ge(h1_out, 16 * B)

        W_TOTAL = (1 + 1 + 4 + 1 + 3 + 9 + 8 + 8) * 16

        @block.gpsimd
        def _(pool):
            nc.gpsimd.memset(query_rows[:, 0, :], MASKED).then_inc(s["const_chain"], 1)
            pool.wait_ge(s["const_chain"], 1)
            nc.gpsimd.memset(query_rows[:, 0, 0:1], 0.0).then_inc(s["const_ready"], 1)
            nc.gpsimd.memset(query_rows[:, 1, :], 0.0).then_inc(s["const_ready"], 1)
            nc.gpsimd.memset(key_rows[:, 0], 0.0).then_inc(s["const_chain"], 1)
            pool.wait_ge(s["const_chain"], 2)
            nc.gpsimd.memset(key_rows[:, 0, :, 0:1], 1.0).then_inc(s["const_ready"], 1)
            nc.gpsimd.memset(key_rows[:, 1], 1.0).then_inc(s["const_ready"], 1)

            def root1(i):
                pool.wait_ge(s["stats1"], i + 1)
                nc.gpsimd.tensor_tensor(var_eps[0:PT, 0:2], mv[0:PT, 0:2, 1], eps[0:PT, 0:2], ALU.add
                                        ).then_inc(s["ln_chain"], 1)
                pool.wait_ge(s["ln_chain"], 2 * i + 1)
                nc.gpsimd.tensor_tensor(rstd[0:PT, 0:2], var_eps[0:PT, 0:2], neg_half[0:PT, :], ALU.pow
                                        ).then_inc(s["rstd1"], 1)

            def root2(i):
                pool.wait_ge(s["stats2"], i + 1)
                nc.gpsimd.tensor_tensor(var_eps[:, 2:4], mv[:, 2:4, 1], eps[0:TOK, 0:2], ALU.add
                                        ).then_inc(s["ln_chain"], 1)
                pool.wait_ge(s["ln_chain"], 2 * i + 2)
                nc.gpsimd.tensor_tensor(rstd[:, 2:4], var_eps[:, 2:4], neg_half[0:TOK, :], ALU.pow
                                        ).then_inc(s["rstd2"], 1)

            def tokens(i, j, b):
                root1(i)
                root2(i)

            pool.wait_ge(s["zeroed"], 1)
            tokens(0, 0, 0)
            tokens(1, 0, 1)
            with pool.Fori(1, B // 2) as j:
                for b in range(2):
                    tokens(2 * j + b, j, b)

        @block.scalar
        def _(act):
            def high(dst, src, sem_name):
                nc.scalar.copy(dst, src).then_inc(s[sem_name], 1)

            def shift(im):
                i, b = im.n, im.par
                act.wait_ge(x_in[b], 16 * X_DMAS * (im.half + 1))
                at_least(act, s["tok_done"], i - 1)
                g = GRID
                nc.scalar.copy(xk[b][:, 6, :, 0:g - 1], xk[b][:, 0, :, 1:g])
                nc.scalar.copy(xk[b][0:64, 7, :, 0:g - 1], xk[b][0:64, 1, :, 1:g])
                nc.scalar.copy(xk[b][64:P, 7, :, 1:g], xk[b][64:P, 4, :, 0:g - 1])
                nc.scalar.copy(xk[b][:, 8, :, 1:g], xk[b][:, 5, :, 0:g - 1]).then_inc(s["x_shift"], 1)

            def inputs(im):
                i = im.n
                act.wait_ge(s["xn_turned"], i + 1)
                at_least(act, s["v_done"], i)
                high(x_h[:], ps_t[:, 0:2 * N].rearrange("p (a n) -> p a n", a=2), "xh_ready")
                at_least(act, s["aug_stored"], 64 * i)
                act.wait_ge(s["qk_done"], 2 * i + 1)
                high(qk_c[:, 0:2, 0, :], ps_a[0:96, 0:2 * N].rearrange("p (a n) -> p a n", a=2), "qh_ready")
                act.wait_ge(s["qk_done"], 2 * i + 2)
                high(qk_c[:, 2:4, 1, :], ps_b[0:96, 0:2 * N].rearrange("p (a n) -> p a n", a=2), "qh_ready")

            def weights(im, before):
                i = im.n
                act.wait_ge(s["max_turned"], i + 1)
                if before.live:
                    act.wait_ge(max_in[before.par], 32 * (before.half + 1))
                nc.scalar.activation(neg_max[:], ps_b[0:HEADS, 0:N], ACT.Copy, scale=-1.0).then_inc(s["max_ready"], 1)
                for g in range(6):
                    act.wait_ge(s["exp_scores"], 6 * i + g + 1)
                    t, pp = g % 2, 2 * (g // 2)
                    nc.scalar.activation(probs[:, t, pp:pp + 2], scores(g % 2), ACT.Exp, scale=SCALE
                                         ).then_inc(s["exp_done"], 1)
                act.wait_ge(s["av_done"], i + 1)
                at_least(act, s["o_tokens"], i)
                nc.scalar.copy(o_t[:, 0:2], ps_a[:, 0:2 * N].rearrange("p (a n) -> p a n", a=2))
                nc.scalar.copy(o_t[:, 2], ps_b[:, 0:N]).then_inc(s["ot_ready"], 1)

            def outputs(im):
                i = im.n
                act.wait_ge(s["o_turned"], i + 1)
                at_least(act, s["proj_done"], i)
                high(o_h[:], ps_t[:, 0:2 * N].rearrange("p (a n) -> p a n", a=2), "oh_ready")

            shift(Image(0, 0, B))
            shift(Image(0, 1, B))
            act.wait_ge(s["w_load"], W_TOTAL)
            high(wqk_h[:], wqk_f[:], "w_split")
            high(wv_h[:], wv_f[:], "w_split")
            high(wp_h[:], wp_f[:], "w_split")

            def step(at):
                if at(0).live:
                    inputs(at(0))
                if at(-2).live:
                    outputs(at(-2))
                if at(2).live:
                    shift(at(2))
                if at(-1).live:
                    weights(at(-1), at(-2))

            run_steps(act, B, step)

        @block.tensor
        def _(pe):
            def contract(out, lhs, rhs):
                for n, (a, c) in enumerate(zip(lhs, rhs)):
                    mm = pe.matmul(out, a, c, start=(n == 0), stop=(n == len(lhs) - 1))
                return mm

            def act_parts(hi, lo, cols):
                return [hi[:, 0, cols], hi[:, 0, cols], lo[:, 0, cols], lo[:, 1, cols], lo[:, 1, cols]]

            def w_parts(hi, lo, cols):
                return [hi[:, 0, cols], lo[:, 0, cols], hi[:, 0, cols], hi[:, 1, cols], lo[:, 1, cols]]

            def project_patches(im, start, stop):
                i, b = im.n, im.par
                if start == 0:
                    pe.wait_ge(x_in[b], 16 * X_DMAS * (im.half + 1))
                    pe.wait_ge(s["x_shift"], i + 1)
                    at_least(pe, s["tok_biased"], i)
                for n in range(start, stop):
                    t, k = n // 12, n % 12
                    x_tile = xk[b][:, k].rearrange("p a c -> p (a c)")[:, t * PT:(t + 1) * PT]
                    mm = pe.matmul(ps_tok[0:PT, t * E:(t + 1) * E], x_tile, w_tok[:, k, :],
                                   start=(k == 0), stop=(k == KC + KH - 1))
                if stop == 24:
                    mm.then_inc(s["tok_done"], 1)

            def turn(src, dst):
                for t in range(2):
                    pe.transpose(dst[:, t * TOK:(t + 1) * TOK], src[:, t, 0:P], ident[0:TOK, 0:TOK])
                    mm = pe.transpose(dst[:, N + t * TOK:N + (t + 1) * TOK],
                                      src[:, t, P:EW],
                                      ident[0:TOK, 0:TOK])
                return mm

            def turn_tokens(im):
                pe.wait_ge(s["xn_ready"], im.n + 1)
                at_least(pe, s["v_ready"], im.n)
                turn(xn[im.par], ps_t).then_inc(s["xn_turned"], 1)

            def queries_keys(i, half):
                if half == 0:
                    pe.wait_ge(s["xh_ready"], i + 1)
                    pe.wait_ge(s["xl_ready"], i + 1)
                    at_least(pe, s["o_ready"], i - 1)
                for m in range(2):
                    c = 2 * half + m
                    mm = contract((ps_a, ps_b)[half][0:96, m * N:(m + 1) * N],
                                  w_parts(wqk_h, wqk_l, slice(96 * c, 96 * c + 96)),
                                  act_parts(x_h, x_l, slice(0, N)))
                mm.then_inc(s["qk_done"], 1)

            def values(i):
                for t in range(2):
                    mm = contract(ps_t[0:TOK, t * E:(t + 1) * E],
                                  act_parts(x_h, x_l, slice(t * TOK, (t + 1) * TOK)),
                                  w_parts(wv_h, wv_l, slice(0, E)))
                mm.then_inc(s["v_done"], 1)

            def max_scores(im, groups):
                i, b = im.n, im.par
                for g in groups:
                    t, pp = g // 3, 2 * (g % 3)
                    if g == 0:
                        pe.wait_ge(q_in[b], 16 * Q_DMAS * (im.half + 1))
                    if g < 2:
                        at_least(pe, s["exp_done"], 6 * (i - 1) + g + 5)
                    else:
                        pe.wait_ge(s["max_read"], 6 * i + g - 1)
                    for a in range(2):
                        for e in range(2):
                            mm = pe.matmul(ps_s[0:TOK, 2 * (g % 2) + a, e * N:(e + 1) * N],
                                           q_aug[b][:, pp + a, t * TOK:(t + 1) * TOK],
                                           k_aug[b][e][:, pp + a, :], start=True, stop=True)
                    mm.then_inc(s["max_scores"], 1)

            def turn_max(i):
                pe.wait_ge(s["max_read"], 6 * i + 6)
                for t in range(2):
                    mm = pe.transpose(ps_b[0:HEADS, t * TOK:(t + 1) * TOK],
                                      maxes[:, t].rearrange("p e a -> p (e a)"), ident[0:TOK, 0:TOK])
                mm.then_inc(s["max_turned"], 1)

            def key_scores(i, b, g):
                t, pp = g % 2, 2 * (g // 2)
                if g >= 2:
                    pe.wait_ge(s["exp_done"], 6 * i + g - 1)
                for a in range(2):
                    for e in range(2):
                        mm = pe.matmul(ps_s[0:TOK, 2 * (g % 2) + a, e * N:(e + 1) * N],
                                       k_aug[b][e][:, pp + a, t * TOK:(t + 1) * TOK],
                                       q_aug[b][:, pp + a, :], start=True, stop=True)
                mm.then_inc(s["exp_scores"], 1)

            def attend(i, b, n):
                pe.wait_ge(s["exp_done"], 6 * i + 2 * n + 2)
                if n == 0:
                    pe.wait_ge(s["v_ready"], i + 1)
                    at_least(pe, s["h1_ready"], i)
                if n == 2:
                    pe.wait_ge(s["max_ready"], i + 1)
                dst = (ps_a[:, 0:N], ps_a[:, N:2 * N], ps_b[:, 0:N])[n]
                for k in range(2):
                    for q in range(4):
                        mm = pe.matmul(dst[32 * q:32 * q + 32], v[b][:, k, 4 * n + q, :],
                                       probs[:, k, 2 * n + q // 2, q % 2, :],
                                       start=(k == 0), stop=(k == 1))
                if n == 2:
                    mm.then_inc(s["av_done"], 1)

            def output_tokens(i):
                pe.wait_ge(s["ot_ready"], i + 1)
                for t in range(2):
                    for n in range(3):
                        mm = pe.transpose((ps_a, ps_b)[t][0:TOK, n * P:(n + 1) * P],
                                          o_t[:, n, t * TOK:(t + 1) * TOK], ident[:, :])
                mm.then_inc(s["o_tokens"], 1)

            def turn_output(i):
                pe.wait_ge(s["o_ready"], i + 1)
                turn(o_n, ps_t).then_inc(s["o_turned"], 1)

            def project_output(i):
                pe.wait_ge(s["oh_ready"], i + 1)
                pe.wait_ge(s["ol_ready"], i + 1)
                for t in range(2):
                    mm = contract(ps_a[0:TOK, t * E:(t + 1) * E],
                                  act_parts(o_h, o_l, slice(t * TOK, (t + 1) * TOK)),
                                  w_parts(wp_h, wp_l, slice(0, E)))
                mm.then_inc(s["proj_done"], 1)

            def step(at):
                new, scored, done, ahead = at(0), at(-1), at(-2), at(1)

                def patches(start, stop):
                    if ahead.live:
                        project_patches(ahead, start, stop)

                def maxima(*groups):
                    if scored.live:
                        max_scores(scored, groups)

                if new.live:
                    turn_tokens(new)
                maxima(2)
                if done.live:
                    output_tokens(done.n)
                patches(0, 8)
                maxima(3)
                if new.live:
                    queries_keys(new.n, 0)
                maxima(4)
                if new.live:
                    queries_keys(new.n, 1)
                if done.live:
                    if not new.live:
                        pe.wait_ge(s["v_ready"], B)
                    turn_output(done.n)
                maxima(5)
                patches(8, 14)
                if new.live and (done.live or scored.live):
                    pe.wait_ge(s["ql_ready"], 2 * new.n + 2)
                if done.live:
                    project_output(done.n)
                if scored.live:
                    turn_max(scored.n)
                patches(14, 24)
                if scored.live:
                    i, b = scored.n, scored.par
                    pe.wait_ge(max_in[b], 32 * (scored.half + 1))
                    key_scores(i, b, 0)
                    key_scores(i, b, 1)
                if new.live:
                    values(new.n)
                if scored.live:
                    key_scores(i, b, 2)
                    key_scores(i, b, 3)
                    attend(i, b, 0)
                    key_scores(i, b, 4)
                    key_scores(i, b, 5)
                    attend(i, b, 1)
                if new.live:
                    max_scores(new, (0, 1))
                if scored.live:
                    attend(i, b, 2)

            pe.wait_ge(s["sums"], 4)
            project_patches(Image(0, 0, B), 0, 24)
            pe.wait_ge(s["w_split"], 6)
            run_steps(pe, B, step)

        @block.vector
        def _(dve):
            for b in range(2):
                nc.vector.memset(xk[b][:, KC:KC + KH].rearrange("p t a c -> p (t a c)"), 0.0)
                for e in range(2):
                    nc.vector.memset(k_aug[b][e][:].rearrange("p a n -> p (a n)").bitcast(F32), 0.0
                                     ).then_inc(s["const_ready"], 1)
                nc.vector.memset(q_aug[b][:].rearrange("p a n -> p (a n)").bitcast(F32), 0.0)
                nc.vector.memset(v[b][:].rearrange("p t h d -> p (t h d)"), 1.0)
            nc.vector.memset(low_half[0:64, :], 0.0)
            nc.vector.memset(low_half[64:P, :], -1.0)
            nc.vector.memset(eps[:], LN_EPS)
            nc.vector.memset(neg_half[:], -0.5).then_inc(s["zeroed"], 1)

            dve.wait_ge(s["w_load"], W_TOTAL)
            for n in range(4):
                at_least(dve, s["sums"], n)
                nc.vector.tensor_tensor(w_tok[:, 0:KC, :], w_tok[:, 0:KC, :], w_add[:, n], ALU.add
                                        ).then_inc(s["sums"], 1)

            dve.wait_ge(s["w_split"], 3)
            for f, hi, lo in ((wqk_f, wqk_h, wqk_l), (wv_f, wv_h, wv_l), (wp_f, wp_h, wp_l)):
                nc.vector.tensor_tensor(lo[:], f[:], hi[:].bitcast(F32), ALU.subtract).then_inc(s["w_split"], 1)

            def moments(src, rows, k):
                for t in range(2):
                    nc.vector.bn_stats(stats[0:rows, k + t, :], src[0:rows, t, :]).then_inc(s["chain"], 1)

            def tokens(im):
                i, q = im.n, im.quad
                dve.wait_ge(s["tok_done"], i + 1)
                nc.vector.tensor_tensor(h_pre[0:PT], ps_tok[0:PT, 0:2 * E].rearrange("p (t e) -> p t e", t=2),
                                        tokb[0:PT].unsqueeze(1).broadcast_to([PT, 2, E]), ALU.add
                                        ).then_inc(s["tok_biased"], 1)
                dve.wait_ge(s["tok_biased"], i + 1)
                moments(h_pre, PT, 0)
                dve.wait_ge(s["chain"], 4 * i + 2)
                nc.vector.memset(wait_pad[:, 0:1], 0.0)
                for t in range(2):
                    ins = nc.vector.bn_aggr(mv[0:PT, t, :], stats[0:PT, t, :])
                ins.then_inc(s["stats1"], 1)
                dve.wait_ge(s["stats1"], i + 1)
                for t in range(2):
                    ins = nc.vector.scalar_tensor_tensor(h_gam[0:PT, t, :], h_pre[0:PT, t, :], mv[0:PT, t, 0:1],
                                                         tokg[0:PT, :], ALU.subtract, ALU.mult)
                ins.then_inc(s["centred"], 1)
                dve.wait_ge(s["centred"], i + 1)
                dve.wait_ge(s["rstd1"], i + 1)
                for t in range(2):
                    ins = nc.vector.scalar_tensor_tensor(h[q][0:PT, t, :], h_gam[0:PT, t, :], rstd[0:PT, t:t + 1],
                                                         tokbeta[0:PT, :], ALU.mult, ALU.add)
                ins.then_inc(s["h_ready"], 1)

            def norm2_moments(im):
                i, b, q = im.n, im.par, im.quad
                dve.wait_ge(s["h_ready"], i + 1)
                dve.wait_ge(txt_in[b], 16 * (im.half + 1))
                moments(h[q], TOK, 2)
                dve.wait_ge(s["chain"], 4 * i + 4)
                nc.vector.memset(wait_pad[:, 0:1], 0.0)
                for t in range(2):
                    ins = nc.vector.bn_aggr(mv[:, 2 + t, :], stats[:, 2 + t, :])
                ins.then_inc(s["stats2"], 1)

            def read_values(im):
                dve.wait_ge(s["v_done"], im.n + 1)
                nc.vector.tensor_copy(v[im.par][:, :, :, 0:HD],
                                      ps_t[0:TOK, 0:2 * E].rearrange("p (t h d) -> p t h d", t=2, h=HEADS)
                                      ).then_inc(s["v_ready"], 1)

            def norm2_scale(im):
                i, b, q = im.n, im.par, im.quad
                dve.wait_ge(s["rstd2"], i + 1)
                at_least(dve, s["xn_turned"], i - 1)
                for t in range(2):
                    ins = nc.vector.tensor_scalar(xn[b][:, t, 0:E], h[q][:, t, :], mv[:, 2 + t, 0:1],
                                                  rstd[:, 2 + t:3 + t], ALU.subtract, ALU.mult)
                ins.then_inc(s["xn_once"], 1)
                dve.wait_ge(s["xn_once"], i + 1)
                nc.vector.tensor_copy(xn[b][:, :, E:EW], xn[b][:, :, P:E]).then_inc(s["xn_ready"], 1)

            def low_parts(src, hi, lo, sem_name):
                nc.vector.tensor_tensor(lo[:, 0, :], src[:, 0:N], hi[:, 0, :].bitcast(F32), ALU.subtract)
                nc.vector.scalar_tensor_tensor(lo[:, 1, :], hi[:, 1, :].bitcast(F32), low_half[:, 0:1],
                                               src[:, N:2 * N], ALU.mult, ALU.add).then_inc(s[sem_name], 1)

            def low_tokens(i):
                dve.wait_ge(s["xh_ready"], i + 1)
                at_least(dve, s["v_done"], i)
                low_parts(ps_t, x_h, x_l, "xl_ready")

            def low_qk(i, m):
                ps, slot = ((ps_a, 1), (ps_b, 0))[m]
                dve.wait_ge(s["qh_ready"], 2 * i + 1 + m)
                nc.vector.tensor_tensor(qk_c[:, 2 * m:2 * m + 2, slot, :],
                                        ps[0:96, 0:2 * N].rearrange("p (a n) -> p a n", a=2),
                                        qk_c[:, 2 * m:2 * m + 2, 1 - slot, :].bitcast(F32),
                                        ALU.subtract).then_inc(s["ql_ready"], 1)

            def read_max(i, g):
                dve.wait_ge(s["max_scores"], 6 * i + g + 1)
                if g == 0:
                    at_least(dve, s["max_turned"], i)
                t, pp = g // 3, 2 * (g % 3)
                nc.vector.tensor_reduce(maxes[:, t, :, pp:pp + 2].rearrange("p e a -> p a e"),
                                        scores(g % 2), AX.X, ALU.max).then_inc(s["max_read"], 1)

            def normalise(i):
                dve.wait_ge(s["o_tokens"], i + 1)
                o = [ps[0:TOK, 0:HEADS * 32].rearrange("p (h d) -> p h d", d=32) for ps in (ps_a, ps_b)]
                for t in range(2):
                    ins = nc.vector.reciprocal(r_sum[:, t], o[t][:, :, HD:HD + 1])
                ins.then_inc(s["recip"], 1)
                dve.wait_ge(s["recip"], i + 1)
                at_least(dve, s["o_turned"], i)
                for t in range(2):
                    ins = nc.vector.tensor_tensor(o_n[:, t, 0:E].rearrange("p (h d) -> p h d", h=HEADS),
                                                  o[t][:, :, 0:HD], r_sum[:, t].broadcast_to([TOK, HEADS, HD]),
                                                  ALU.mult)
                ins.then_inc(s["o_once"], 1)
                dve.wait_ge(s["o_once"], i + 1)
                nc.vector.tensor_copy(o_n[:, :, E:EW], o_n[:, :, P:E]).then_inc(s["o_ready"], 1)

            def low_o(i):
                dve.wait_ge(s["oh_ready"], i + 1)
                at_least(dve, s["proj_done"], i)
                low_parts(ps_t, o_h, o_l, "ol_ready")

            def residual(im):
                i = im.n
                dve.wait_ge(s["proj_done"], i + 1)
                at_least(dve, h1_out, 16 * i)
                nc.vector.tensor_tensor(h1[:], ps_a[0:TOK, 0:2 * E].rearrange("p (t e) -> p t e", t=2),
                                        h[im.quad][:], ALU.add).then_inc(s["h1_ready"], 1)

            def step(at):
                new, scored, done, ahead = at(0), at(-1), at(-2), at(1)

                def maximum(g):
                    if scored.live:
                        read_max(scored.n, g)

                maximum(0)
                if new.live:
                    low_tokens(new.n)
                maximum(1)
                if done.live:
                    normalise(done.n)
                maximum(2)
                maximum(3)
                if new.live:
                    low_qk(new.n, 0)
                maximum(4)
                if new.live:
                    low_qk(new.n, 1)
                if done.live:
                    low_o(done.n)
                maximum(5)
                if done.live:
                    residual(done)
                if ahead.live:
                    tokens(ahead)
                    norm2_moments(ahead)
                if new.live:
                    read_values(new)
                if ahead.live:
                    norm2_scale(ahead)

            tokens(Image(0, 0, B))
            norm2_moments(Image(0, 0, B))
            norm2_scale(Image(0, 0, B))
            run_steps(dve, B, step)


def stage_experts(nc, B, h1_d, w1, b1, w2, b2, down_w, down_b, up_w, gamma, beta, ident_d, out):
    PAIR = 4
    NN = PAIR * TOK
    steps = B // 2
    with ExitStack() as ctx:
        def sb(name, shape, dt=F32):
            return ctx.enter_context(nc.sbuf_tensor(name, shape, dt))

        def psum(name, shape):
            return ctx.enter_context(nc.psum_tensor(name, shape, F32))

        def sem(name):
            return ctx.enter_context(nc.semaphore(name))

        ident = sb("ident2", [P, P])
        low_half = sb("low_half2", [P, 1])
        neg_half = sb("neg_half2", [P, PAIR])
        eps = sb("eps2", [P, PAIR])
        wait_pad = sb("wait_pad2", [P, 1])
        rank = sb("rank", [P, PAIR, EXPERTS])
        wd_f = sb("wd_f", [P, 2, EXPERTS * DFF])
        wd_h, wd_l = sb("wd_h", [P, 2, EXPERTS * DFF], F32R), sb("wd_l", [P, 2, EXPERTS * DFF], F32R)
        w1_f = sb("w1_f", [P, 2, W1N])
        w1_h, w1_l = sb("w1_h", [P, 2, W1N], F32R), sb("w1_l", [P, 2, W1N], F32R)
        wu_f = sb("wu_f", [P, MT, E])
        wu_h, wu_l = sb("wu_h", [P, MT, E], F32R), sb("wu_l", [P, MT, E], F32R)
        w2s = sb("w2s", [W1N, EXPERTS])
        b1s = sb("b1s", [W1N, 1])
        b2s = sb("b2s", [P, EXPERTS])
        bd = sb("bd", [P, MT])
        gam = sb("gam", [P, E])
        bet = sb("bet", [P, E])

        hin = [sb(f"hin{b}", [TOK, PAIR, E]) for b in range(2)]
        hres = [sb(f"hres{b}", [TOK, PAIR, E]) for b in range(2)]
        x2 = [sb(f"x2{b}", [TOK, PAIR, EW]) for b in range(2)]
        x_h = [sb(f"fx_h{b}", [P, 2, NN], F32R) for b in range(2)]
        x_l = [sb(f"fx_l{b}", [P, 2, NN], F32R) for b in range(2)]
        gates = [sb(f"gates{b}", [TOK, PAIR, EXPERTS]) for b in range(2)]
        u = sb("u", [W1N, NN])
        z = [sb(f"z{b}", [P, 2, NN]) for b in range(2)]
        z_h = [sb(f"z_h{b}", [P, 2, NN], F32R) for b in range(2)]
        z_l = [sb(f"z_l{b}", [P, 2, NN], F32R) for b in range(2)]
        acc = [sb(f"acc{b}", [TOK, PAIR, E]) for b in range(2)]
        y = sb("y", [TOK, PAIR, E])
        y_g = sb("y_g", [TOK, PAIR, E])
        y_b = sb("y_b", [TOK, PAIR, E])
        y_o = sb("y_o", [TOK, PAIR, E])
        stats = sb("fstats", [TOK, 2, PAIR, 6])
        mv = sb("fmv", [TOK, 2, PAIR, 2])
        var_eps = sb("fvar", [TOK, 2, PAIR])
        rstd = sb("frstd", [TOK, 2, PAIR])
        r8 = [sb(f"r8_{n}", [TOK, PAIR, EXPERTS]) for n in range(9)]
        r1 = [sb(f"r1_{n}", [TOK, PAIR, 1]) for n in range(9)]

        ps_d = psum("ps_d", [P, 2, 512])
        ps_u = psum("ps_u", [P, 4, 512])
        ps_x = psum("ps_x", [P, 2, 512])

        names = """w_load down_load up_load consts w_split w_low ln_stats ln_root x_once x_ready turned xh_ready xl_ready
            w1_done u_ready logits_done route_in route_exp route_chain gates_ready
            down_done z_ready zh_ready zl_ready up_done acc_done y_stats y_root y_ready y_chain out_ready
            ln_chain ln_pool""".split()
        s = {n: sem("f_" + n) for n in names}
        h_in = [sem(f"f_h_in{b}") for b in range(2)]
        hres_in = [sem(f"f_hres_in{b}") for b in range(2)]
        stored = sem("f_stored")
        LOADS = 7 * 16
        ROUTE = 21

        block = ctx.enter_context(nc.Block())

        @block.sync
        def _(sp):
            def load(j, b):
                at_least(sp, s["x_once"], j - 1)
                for a in range(2):
                    sp.dma_start(hin[b][:, 2 * a:2 * a + 2, :], h1_d[2 * j + a]).then_inc(h_in[b], 16)

            def load_residual(j, b):
                at_least(sp, s["out_ready"], j - 1)
                for a in range(2):
                    sp.dma_start(hres[b][:, 2 * a:2 * a + 2, :], h1_d[2 * j + a]).then_inc(hres_in[b], 16)

            load(0, 0)

            def w(dst, src, name):
                sp.dma_start(dst, src).then_inc(s[name], 16)

            def w_twice(f, src, name):
                w(f[:, 0, :], src[0:P, :], name)
                w(f[0:64, 1, :], src[P:E, :], name)
                w(f[64:P, 1, :], src[P:E, :], name)

            w(ident[:, :], ident_d, "w_load")
            w_twice(w1_f, w1, "w_load")
            w(b1s[:, :], b1, "w_load")
            w(w2s[:, :], w2, "w_load")
            w(b2s[:, :], b2, "w_load")
            w_twice(wd_f, down_w, "down_load")
            load(1, 1)
            w(bd[:, :], down_b, "up_load")
            w(wu_f[:], up_w.rearrange("(m p) e -> p m e", p=P), "up_load")
            w(gam[:, :], gamma, "up_load")
            w(bet[:, :], beta, "up_load")
            load_residual(0, 0)
            load_residual(1, 1)
            load(2, 0)
            load(3, 1)

            def store(j):
                sp.wait_ge(s["out_ready"], j + 1)
                for a in range(2):
                    t = slice(2 * a, 2 * a + 2)
                    sp.dma_start(out[2 * j + a, 0:NP].rearrange("(t p) e -> p t e", p=PT),
                                 y_o[0:PT, t, :]).then_inc(stored, 16)
                    sp.dma_start(out[2 * j + a, NP:N].rearrange("(t p) e -> p t e", p=TT),
                                 y_o[PT:TOK, t, :]).then_inc(stored, 16)

            def step(j, b, more=True):
                store(j)
                if more:
                    load_residual(j + 2, b)
                    load(j + 4, b)

            with sp.Fori(0, steps // 2 - 2) as jj:
                step(2 * jj, 0)
                step(2 * jj + 1, 1)
            store(steps - 4)
            load_residual(steps - 2, 0)
            store(steps - 3)
            load_residual(steps - 1, 1)
            store(steps - 2)
            store(steps - 1)
            sp.wait_ge(stored, 64 * steps)

        @block.gpsimd
        def _(pool):
            def root(n, src, dst, pair, count):
                pool.wait_ge(s[src], pair + 1)
                nc.gpsimd.tensor_tensor(var_eps[:, n], mv[:, n, :, 1], eps[0:TOK, :], ALU.add
                                        ).then_inc(s["ln_pool"], 1)
                pool.wait_ge(s["ln_pool"], count + 1)
                nc.gpsimd.tensor_tensor(rstd[:, n], var_eps[:, n], neg_half[0:TOK, :], ALU.pow
                                        ).then_inc(s[dst], 1)

            def finish(j, jj, b, count):
                root(1, "y_stats", "y_root", j, count)
                pool.wait_ge(s["y_ready"], j + 1)
                nc.gpsimd.tensor_tensor(y_g[:], y[:], gam[0:TOK].unsqueeze(1).broadcast_to([TOK, PAIR, E]),
                                        ALU.mult).then_inc(s["y_chain"], 1)
                pool.wait_ge(s["y_chain"], 2 * j + 1)
                nc.gpsimd.tensor_tensor(y_b[:], y_g[:], bet[0:TOK].unsqueeze(1).broadcast_to([TOK, PAIR, E]),
                                        ALU.add).then_inc(s["y_chain"], 1)
                pool.wait_ge(s["y_chain"], 2 * j + 2)
                pool.wait_ge(hres_in[b], 32 * (jj + 1))
                at_least(pool, stored, 64 * j)
                nc.gpsimd.tensor_tensor(y_o[:], y_b[:], hres[b][:], ALU.add).then_inc(s["out_ready"], 1)

            pool.wait_ge(s["consts"], 1)
            root(0, "ln_stats", "ln_root", 0, 0)
            root(0, "ln_stats", "ln_root", 1, 1)
            pool.wait_ge(s["up_load"], 4 * 16)
            root(0, "ln_stats", "ln_root", 2, 2)
            finish(0, 0, 0, 3)
            root(0, "ln_stats", "ln_root", 3, 4)
            with pool.Fori(1, steps // 2 - 1) as jj:
                finish(2 * jj - 1, jj - 1, 1, 4 * jj + 1)
                root(0, "ln_stats", "ln_root", 2 * jj + 2, 4 * jj + 2)
                finish(2 * jj, jj, 0, 4 * jj + 3)
                root(0, "ln_stats", "ln_root", 2 * jj + 3, 4 * jj + 4)
            finish(steps - 3, steps // 2 - 2, 1, 2 * steps - 3)
            finish(steps - 2, steps // 2 - 1, 0, 2 * steps - 2)
            finish(steps - 1, steps // 2 - 1, 1, 2 * steps - 1)

        @block.scalar
        def _(act):
            act.wait_ge(s["w_load"], LOADS)
            nc.scalar.copy(w1_h[:], w1_f[:]).then_inc(s["w_split"], 1)

            def high_x(j, b):
                act.wait_ge(s["turned"], j + 1)
                at_least(act, s["down_done"], 16 * (j - 1))
                nc.scalar.copy(x_h[b][:], ps_x[:, :, 0:NN]).then_inc(s["xh_ready"], 1)

            def hidden_router(j):
                act.wait_ge(s["w1_done"], j + 1)
                at_least(act, s["logits_done"], j)
                nc.scalar.activation(u[:, :], ps_x[0:W1N, 0, 0:NN], ACT.Gelu, bias=b1s[:, 0:1]
                                     ).then_inc(s["u_ready"], 1)

            def exp_router(j):
                act.wait_ge(s["route_in"], j + 1)
                nc.scalar.activation(r8[2][:], r8[1][:], ACT.Exp).then_inc(s["route_exp"], 1)

            def hidden(j, e):
                at_least(act, s["up_done"], 8 * j + e - 1)
                for n in range(2):
                    m = 2 * e + n
                    act.wait_ge(s["down_done"], 16 * j + m + 1)
                    nc.scalar.activation(z[e % 2][:, n, :], ps_d[:, n, 0:NN], ACT.Gelu, bias=bd[:, m:m + 1]
                                         ).then_inc(s["z_ready"], 1)
                    act.wait_ge(s["z_ready"], 16 * j + m + 1)
                    nc.scalar.copy(z_h[e % 2][:, n, :], z[e % 2][:, n, :]).then_inc(s["zh_ready"], 1)

            def step(j, b, last=False):
                for e in range(EXPERTS):
                    hidden(j, e)
                    if not last and e == 2:
                        high_x(j + 1, 1 - b)
                    if not last and e == 3:
                        hidden_router(j + 1)
                    if not last and e == 5:
                        exp_router(j + 1)

            high_x(0, 0)
            act.wait_ge(s["down_load"], 3 * 16)
            nc.scalar.copy(wd_h[:], wd_f[:]).then_inc(s["w_split"], 1)
            hidden_router(0)
            act.wait_ge(s["up_load"], 4 * 16)
            nc.scalar.copy(wu_h[:], wu_f[:]).then_inc(s["w_split"], 1)
            exp_router(0)
            step(0, 0)
            step(1, 1)
            with act.Fori(1, steps // 2 - 1) as jj:
                step(2 * jj, 0)
                step(2 * jj + 1, 1)
            step(steps - 2, 0)
            step(steps - 1, 1, last=True)

        @block.tensor
        def _(pe):
            def contract(out_, lhs, rhs):
                for n, (a, c) in enumerate(zip(lhs, rhs)):
                    mm = pe.matmul(out_, a, c, start=(n == 0), stop=(n == len(lhs) - 1))
                return mm

            def x_parts(b):
                hi, lo = x_h[b], x_l[b]
                return [hi[:, 0, :], hi[:, 0, :], lo[:, 0, :], lo[:, 1, :], lo[:, 1, :]]

            def w_parts(hi, lo, cols):
                return [hi[:, 0, cols], lo[:, 0, cols], hi[:, 0, cols], hi[:, 1, cols], lo[:, 1, cols]]

            def turn(j, b):
                pe.wait_ge(s["x_ready"], j + 1)
                at_least(pe, s["route_in"], j)
                for t in range(PAIR):
                    pe.transpose(ps_x[:, 0, t * TOK:(t + 1) * TOK], x2[b][:, t, 0:P], ident[0:TOK, 0:TOK])
                    mm = pe.transpose(ps_x[:, 1, t * TOK:(t + 1) * TOK],
                                      x2[b][:, t, P:EW],
                                      ident[0:TOK, 0:TOK])
                mm.then_inc(s["turned"], 1)

            def router_hidden(j, b):
                pe.wait_ge(s["xh_ready"], j + 1)
                pe.wait_ge(s["xl_ready"], j + 1)
                contract(ps_x[0:W1N, 0, 0:NN], w_parts(w1_h, w1_l, slice(0, W1N)), x_parts(b)
                         ).then_inc(s["w1_done"], 1)

            def logits(j):
                pe.wait_ge(s["u_ready"], j + 1)
                for t in range(PAIR):
                    mm = pe.matmul(ps_x[0:TOK, 1, t * EXPERTS:(t + 1) * EXPERTS], u[:, t * TOK:(t + 1) * TOK],
                                   w2s[:, :], start=True, stop=True)
                mm.then_inc(s["logits_done"], 1)

            def down(j, b, e):
                for n in range(2):
                    m = 2 * e + n
                    at_least(pe, s["z_ready"], 16 * j + m - 1)
                    contract(ps_d[:, n, 0:NN], w_parts(wd_h, wd_l, slice(m * P, (m + 1) * P)), x_parts(b)
                             ).then_inc(s["down_done"], 1)

            def up(j, e):
                pe.wait_ge(s["zl_ready"], 16 * j + 2 * e + 2)
                at_least(pe, s["acc_done"], 8 * j + e - 1)
                for t in range(PAIR):
                    hi, lo = (part[e % 2][:, :, t * TOK:(t + 1) * TOK] for part in (z_h, z_l))
                    w_hi, w_lo = wu_h[:, 2 * e:2 * e + 2], wu_l[:, 2 * e:2 * e + 2]
                    mm = contract(ps_u[0:TOK, 2 * (e % 2) + t // 2, (t % 2) * E:(t % 2 + 1) * E],
                                  [hi[:, 0], hi[:, 0], lo[:, 0], hi[:, 1], hi[:, 1], lo[:, 1]],
                                  [w_hi[:, 0], w_lo[:, 0], w_hi[:, 0], w_hi[:, 1], w_lo[:, 1], w_hi[:, 1]])
                mm.then_inc(s["up_done"], 1)

            def step(j, b, first=False, last=False):
                if first:
                    pe.wait_ge(s["w_low"], 2)
                for e in range(EXPERTS):
                    down(j, b, e)
                    if first and e == 1:
                        pe.wait_ge(s["w_low"], 3)
                    if e:
                        up(j, e - 1)
                    elif not first:
                        up(j - 1, EXPERTS - 1)
                    if not last and e == 2:
                        turn(j + 1, 1 - b)
                    if not last and e == 3:
                        router_hidden(j + 1, 1 - b)
                    if not last and e == 4:
                        logits(j + 1)

            pe.wait_ge(s["w_load"], LOADS)
            turn(0, 0)
            pe.wait_ge(s["w_low"], 1)
            router_hidden(0, 0)
            logits(0)
            step(0, 0, first=True)
            step(1, 1)
            with pe.Fori(1, steps // 2 - 1) as jj:
                step(2 * jj, 0)
                step(2 * jj + 1, 1)
            step(steps - 2, 0)
            step(steps - 1, 1, last=True)
            up(steps - 1, EXPERTS - 1)

        @block.vector
        def _(dve):
            nc.vector.memset(low_half[0:64, :], 0.0)
            nc.vector.memset(low_half[64:P, :], -1.0)
            for e in range(EXPERTS):
                nc.vector.memset(rank[:, :, e:e + 1], float(EXPERTS - e))
            nc.vector.memset(eps[:], LN_EPS)
            nc.vector.memset(neg_half[:], -0.5).then_inc(s["consts"], 1)

            def moments(n, src, count, sem_name):
                for t in range(PAIR):
                    nc.vector.bn_stats(stats[:, n, t, :], src[:, t, :]).then_inc(s["ln_chain"], 1)
                dve.wait_ge(s["ln_chain"], count + PAIR)
                nc.vector.memset(wait_pad[:, 0:1], 0.0)
                for t in range(PAIR):
                    ins = nc.vector.bn_aggr(mv[:, n, t, :], stats[:, n, t, :])
                ins.then_inc(s[sem_name], 1)

            def scale(dst, src, n):
                for t in range(PAIR):
                    ins = nc.vector.tensor_scalar(dst[:, t, 0:E], src[:, t, :], mv[:, n, t, 0:1],
                                                  rstd[:, n, t:t + 1], ALU.subtract, ALU.mult)
                return ins

            def norm_moments(jj, b, count):
                dve.wait_ge(h_in[b], 32 * (jj + 1))
                moments(0, hin[b], PAIR * count, "ln_stats")

            def norm_scale(j, b):
                dve.wait_ge(s["ln_root"], j + 1)
                at_least(dve, s["turned"], j - 1)
                scale(x2[b], hin[b], 0).then_inc(s["x_once"], 1)
                dve.wait_ge(s["x_once"], j + 1)
                nc.vector.tensor_copy(x2[b][:, :, E:EW], x2[b][:, :, P:E]).then_inc(s["x_ready"], 1)

            def low_x(j, b):
                dve.wait_ge(s["xh_ready"], j + 1)
                nc.vector.tensor_tensor(x_l[b][:, 0, :], ps_x[:, 0, 0:NN], x_h[b][:, 0, :].bitcast(F32),
                                        ALU.subtract)
                nc.vector.scalar_tensor_tensor(x_l[b][:, 1, :], x_h[b][:, 1, :].bitcast(F32), low_half[:, 0:1],
                                               ps_x[:, 1, 0:NN], ALU.mult, ALU.add).then_inc(s["xl_ready"], 1)

            def logits_in(j):
                dve.wait_ge(s["logits_done"], j + 1)
                count = ROUTE * j

                nc.vector.tensor_tensor(r8[0][:], ps_x[0:TOK, 1, 0:PAIR * EXPERTS].rearrange(
                    "p (t e) -> p t e", t=PAIR), b2s[0:TOK].unsqueeze(1).broadcast_to([TOK, PAIR, EXPERTS]),
                    ALU.add).then_inc(s["route_chain"], 1)
                dve.wait_ge(s["route_chain"], count + 1)
                nc.vector.tensor_reduce(r1[0][:, :, 0], r8[0][:], AX.X, ALU.max).then_inc(s["route_chain"], 1)
                dve.wait_ge(s["route_chain"], count + 2)
                nc.vector.tensor_tensor(r8[1][:], r8[0][:], wide(r1[0]), ALU.subtract).then_inc(s["route_in"], 1)

            def wide(a):
                return a[:].broadcast_to([TOK, PAIR, EXPERTS])

            def link(n, ins):
                ins.then_inc(s["route_chain"], 1)
                dve.wait_ge(s["route_chain"], n)

            tt, red = nc.vector.tensor_tensor, nc.vector.tensor_reduce

            def route_largest(j):
                dve.wait_ge(s["route_exp"], j + 1)
                n = ROUTE * j + 2
                link(n + 1, red(r1[1][:, :, 0], r8[2][:], AX.X, ALU.add))
                link(n + 2, nc.vector.reciprocal(r1[2][:], r1[1][:]))
                link(n + 3, tt(r8[3][:], r8[2][:], wide(r1[2]), ALU.mult))
                link(n + 4, red(r1[3][:, :, 0], r8[3][:], AX.X, ALU.max))
                link(n + 5, tt(r8[4][:], r8[3][:], wide(r1[3]), ALU.is_ge))
                link(n + 6, tt(r8[5][:], r8[4][:], rank[0:TOK], ALU.mult))
                link(n + 7, red(r1[4][:, :, 0], r8[5][:], AX.X, ALU.max))
                link(n + 8, tt(r8[4][:], r8[5][:], wide(r1[4]), ALU.is_ge))

            def route_gates(j, b):
                at_least(dve, s["acc_done"], 8 * (j - 1))
                n = ROUTE * j + 10
                link(n + 1, nc.vector.scalar_tensor_tensor(r8[6][:], r8[4][:], -2.0, r8[3][:], ALU.mult, ALU.add))
                link(n + 2, red(r1[5][:, :, 0], r8[6][:], AX.X, ALU.max))
                link(n + 3, tt(r8[5][:], r8[6][:], wide(r1[5]), ALU.is_ge))
                link(n + 4, tt(r8[7][:], r8[5][:], rank[0:TOK], ALU.mult))
                link(n + 5, red(r1[6][:, :, 0], r8[7][:], AX.X, ALU.max))
                link(n + 6, tt(r8[5][:], r8[7][:], wide(r1[6]), ALU.is_ge))
                link(n + 7, tt(r8[6][:], r8[4][:], r8[5][:], ALU.add))
                link(n + 8, tt(r8[8][:], r8[6][:], r8[3][:], ALU.mult))
                link(n + 9, red(r1[7][:, :, 0], r8[8][:], AX.X, ALU.add))
                link(n + 10, nc.vector.tensor_scalar(r1[8][:], r1[7][:], GATE_EPS, None, ALU.add))
                link(n + 11, nc.vector.reciprocal(r1[2][:], r1[8][:]))
                tt(gates[b][:], r8[8][:], wide(r1[2]), ALU.mult).then_inc(s["gates_ready"], 1)

            def low_hidden(j, e):
                for n in range(2):
                    dve.wait_ge(s["zh_ready"], 16 * j + 2 * e + n + 1)
                    nc.vector.tensor_tensor(z_l[e % 2][:, n, :], z[e % 2][:, n, :],
                                            z_h[e % 2][:, n, :].bitcast(F32), ALU.subtract
                                            ).then_inc(s["zl_ready"], 1)

            def gather(j, b, e, last=False):
                if e < EXPERTS - 1:
                    low_hidden(j, e + 1)
                elif not last:
                    low_hidden(j + 1, 0)
                dve.wait_ge(s["up_done"], 8 * j + e + 1)
                if e == 0:
                    dve.wait_ge(s["gates_ready"], j + 1)
                else:
                    dve.wait_ge(s["acc_done"], 8 * j + e)
                for t in range(PAIR):
                    base = x2[b] if e == 0 else acc[b]
                    ins = nc.vector.scalar_tensor_tensor(
                        acc[b][:, t, :], ps_u[0:TOK, 2 * (e % 2) + t // 2, (t % 2) * E:(t % 2 + 1) * E],
                        gates[b][:, t, e:e + 1], base[:, t, 0:E], ALU.mult, ALU.add)
                ins.then_inc(s["acc_done"], 1)

            def result_moments(j, b, count):
                dve.wait_ge(s["acc_done"], 8 * j + 8)
                moments(1, acc[b], PAIR * count, "y_stats")

            def result_scale(j, b):
                dve.wait_ge(s["y_root"], j + 1)
                at_least(dve, s["y_chain"], 2 * j)
                scale(y, acc[b], 1).then_inc(s["y_ready"], 1)

            def step(j, jj, b, first=False, last=False, norm=True):
                if not first:
                    result_moments(j - 1, 1 - b, 2 * j + 1 - (1 if last else 0))
                gather(j, b, 0)
                if not first:
                    result_scale(j - 1, 1 - b)
                gather(j, b, 1)
                if not last:
                    low_x(j + 1, 1 - b)
                gather(j, b, 2)
                if norm:
                    norm_moments(jj + 1, b, 2 if first else 2 * j + 2)
                gather(j, b, 3)
                if not last:
                    logits_in(j + 1)
                if norm:
                    norm_scale(j + 2, b)
                gather(j, b, 4)
                gather(j, b, 5)
                if not last:
                    route_largest(j + 1)
                gather(j, b, 6)
                if not last:
                    route_gates(j + 1, 1 - b)
                gather(j, b, 7, last=last)

            norm_moments(0, 0, 0)
            norm_scale(0, 0)

            def low_weights(n, f, hi, lo):
                dve.wait_ge(s["w_split"], n)
                nc.vector.tensor_tensor(lo[:], f[:], hi[:].bitcast(F32), ALU.subtract).then_inc(s["w_low"], 1)

            low_weights(1, w1_f, w1_h, w1_l)
            low_x(0, 0)
            norm_moments(0, 1, 1)
            norm_scale(1, 1)
            low_weights(2, wd_f, wd_h, wd_l)
            logits_in(0)
            low_weights(3, wu_f, wu_h, wu_l)
            route_largest(0)
            route_gates(0, 0)
            low_hidden(0, 0)
            step(0, 0, 0, first=True)
            step(1, 0, 1)
            with dve.Fori(1, steps // 2 - 1) as jj:
                step(2 * jj, jj, 0)
                step(2 * jj + 1, jj, 1)
            step(steps - 2, steps // 2 - 1, 0, norm=False)
            step(steps - 1, steps // 2 - 1, 1, last=True, norm=False)
            result_moments(steps - 1, 1, 2 * steps - 1)
            result_scale(steps - 1, 1)


def early_fusion(nc, x_k, txt, w_center, w_halo, tok_b, tok_g, tok_beta, wqk, wv, wproj,
                 w1, b1, w2, b2, down_w, down_b, up_w, gamma, beta, ident, out):
    B = x_k.shape[0]
    aug_d = nc.dram_tensor("aug_d", (2, 4, 34, PAIRS, N), F32, kind="Internal").ap()
    h1_d = nc.dram_tensor("h1_d", (B, TOK, 2, E), F32, kind="Internal").ap()
    stage_attention(nc, B, x_k, txt, w_center, w_halo, tok_b, tok_g, tok_beta, wqk, wv, wproj, ident, aug_d, h1_d)
    stage_experts(nc, B, h1_d, w1, b1, w2, b2, down_w, down_b, up_w, gamma, beta, ident, out)


def kernel(**inputs):
    import numpy as np
    import concourse.bacc as bacc
    from concourse.bass_utils import run_bass_kernel_spmd

    a = {k.removeprefix("L0_"): np.asarray(v) for k, v in inputs.items()}
    B = a["x"].shape[0]
    rows = KC * P
    x_k = a["x"].reshape(B, 3, GRID, 16, GRID, 16).transpose(0, 5, 1, 3, 2, 4).reshape(B, rows, NP)
    w5 = a["tok_proj_w"].reshape(E, 16, 16, 5, 3).transpose(3, 2, 4, 1, 0)
    center = np.zeros_like(w5)
    center[0] = w5[0]
    center[1][:12] = w5[1][4:]
    center[2][:, :, :12] = w5[2][:, :, 4:]
    center[3][4:] = w5[3][:12]
    center[4][:, :, 4:] = w5[4][:, :, :12]
    right, left = w5[3].reshape(rows, E), w5[1].reshape(rows, E)
    halo = np.concatenate([right[576:768], left[0:192],
                           w5[2][:, :, 0:4].reshape(192, E), w5[4][:, :, 12:16].reshape(192, E)])
    wq = a["attn_Wq"].reshape(PAIRS, 2, HD, E).transpose(1, 2, 0, 3)
    wkv = a["attn_Wkv"].reshape(HEADS, 2, HD, E)
    wk = wkv[:, 0].reshape(PAIRS, 2, HD, E).transpose(1, 2, 0, 3)
    wqk = np.concatenate([wq.reshape(E, E), wk.reshape(E, E)]).T
    wide = lambda v: np.broadcast_to(v, (P, v.shape[-1]))
    named = {
        "x_k": x_k, "txt": a["txt"], "w_center": center.reshape(5, rows, E), "w_halo": halo,
        "tok_b": wide(a["tok_proj_b"]), "tok_g": wide(a["tok_gamma"]), "tok_beta": wide(a["tok_beta"]),
        "wqk": wqk, "wv": wkv[:, 1].reshape(E, E).T, "wproj": a["attn_Wproj"].T,
        "w1": a["ffn_w1"], "b1": a["ffn_b1"].reshape(W1N, 1), "w2": a["ffn_w2"], "b2": wide(a["ffn_b2"]),
        "down_w": a["ffn_down_w"].transpose(1, 0, 2).reshape(E, EXPERTS * DFF),
        "down_b": a["ffn_down_b"].reshape(MT, P).T, "up_w": a["ffn_up_w"].reshape(EXPERTS * DFF, E),
        "gamma": wide(a["ffn_gamma"]), "beta": wide(a["ffn_beta"]), "ident": np.eye(P, dtype=np.float32),
    }
    nc = bacc.Bacc("TRN2", target_bir_lowering=False, num_devices=1)
    arrays, args = {}, []
    for name, value in named.items():
        arrays[f"in_{name}"] = np.ascontiguousarray(value)
        args.append(nc.dram_tensor(f"in_{name}", value.shape, F32, kind="ExternalInput").ap())
    args.append(nc.dram_tensor("out", (B, N, E), F32, kind="ExternalOutput").ap())
    early_fusion(nc, *args)
    return run_bass_kernel_spmd(nc, [arrays], core_ids=[0]).results[0]["out"]
```
